# Optimizing a Trainium2 kernel written in Bass

```python
import numpy as np
import jax
import jax.numpy as jnp

def _softmax(x, axis=-1):
    return jax.nn.softmax(x, axis=axis)

def _gelu(x):
    return jax.nn.gelu(x, approximate=True)

def _silu(x):
    return jax.nn.silu(x)

def _sigmoid(x):
    return jax.nn.sigmoid(x)

def _layernorm(x, axis=-1, eps=1e-05):
    m = jnp.mean(x, axis=axis, keepdims=True)
    v = jnp.var(x, axis=axis, keepdims=True)
    return (x - m) / jnp.sqrt(v + eps)

def _scatter_add(tgt, idx, src, axis=0):
    return tgt.at[idx].add(src)

def _segment_sum(src, seg, n):
    return jax.ops.segment_sum(src, seg, n)
kernel_name = 'mk_prb_d1_jaxref_r4_a33c2a'

def setup_inputs(seed: int=0):
    np.random.seed(seed)
    _w = jnp.asarray

    def _L0_attn_setup():
        import jax, jax.numpy as jnp
        import numpy as np
        from jax import lax
        B, S, D = (8, 256, 256)
        DH = D // 2
        H = 8
        DK = DH // H
        DFF = 4 * D
        ALPHA, BETA = (0.1, 0.1)
        EPS = 1e-05
        PARAM_SPECS = [('wq1', (DH, DH)), ('bq1', (DH,)), ('wk1', (DH, DH)), ('bk1', (DH,)), ('wv1', (DH, DH)), ('bv1', (DH,)), ('wo1', (DH, DH)), ('bo1', (DH,)), ('wq2', (DH, DH)), ('bq2', (DH,)), ('wk2', (DH, DH)), ('bk2', (DH,)), ('wv2', (DH, DH)), ('bv2', (DH,)), ('wo2', (DH, DH)), ('bo2', (DH,)), ('g1', (DH,)), ('be1', (DH,)), ('g2', (DH,)), ('be2', (DH,)), ('w_ff1', (DFF, D)), ('b_ff1', (DFF,)), ('w_ff2', (D, DFF)), ('b_ff2', (D,)), ('g_ff', (D,)), ('be_ff', (D,))]

        def layernorm(x, g, b):
            m = jnp.mean(x, axis=-1, keepdims=True)
            v = jnp.mean(jnp.square(x - m), axis=-1, keepdims=True)
            return (x - m) * lax.rsqrt(v + EPS) * g + b

        def mha(xin, wq, bq, wk, bk, wv, bv, wo, bo):
            b, s, _ = xin.shape
            q = (xin @ wq.T + bq).reshape(b, s, H, DK)
            k = (xin @ wk.T + bk).reshape(b, s, H, DK)
            v = (xin @ wv.T + bv).reshape(b, s, H, DK)
            scores = jnp.einsum('bshd,bthd->bhst', q, k) * (1.0 / np.sqrt(DK).astype(np.float32))
            a = jax.nn.softmax(scores, axis=-1)
            o = jnp.einsum('bhst,bthd->bshd', a, v).reshape(b, s, DH)
            return o @ wo.T + bo

        def holt(x, alpha, beta):
            x0 = x[:, 0]

            def step(carry, xt):
                level, trend = carry
                nl = alpha * xt + (1.0 - alpha) * (level + trend)
                nt = beta * (nl - level) + (1.0 - beta) * trend
                return ((nl, nt), nl)
            _, lv = lax.scan(step, (x0, jnp.zeros_like(x0)), jnp.swapaxes(x[:, 1:], 0, 1))
            return jnp.concatenate([x0[:, None], jnp.swapaxes(lv, 0, 1)], axis=1)
        key = jax.random.key(seed)
        inp = {'x': jax.random.normal(jax.random.fold_in(key, 0), (B, S, D), jnp.float32)}
        for i, (name, shape) in enumerate(PARAM_SPECS):
            k = jax.random.fold_in(key, i + 1)
            if name.startswith('g'):
                inp[name] = jnp.ones(shape, jnp.float32)
            elif name.startswith('b'):
                inp[name] = jnp.zeros(shape, jnp.float32)
            else:
                inp[name] = jax.random.normal(k, shape, jnp.float32) * 0.02
        return inp
    _L0_attn_in = _L0_attn_setup()

    def _L0_ffn_setup():
        import jax, jax.numpy as jnp
        import numpy as np
        HIDDEN = 256
        INTER = 1024
        key = jax.random.key(seed)
        k1, k2, k3, k4, k5 = jax.random.split(key, 5)
        hidden_states = jax.random.normal(k1, (4, 512, HIDDEN), dtype=jnp.float32)
        W1 = jax.random.normal(k2, (HIDDEN, INTER), dtype=jnp.float32) * (1.0 / np.sqrt(HIDDEN))
        b1 = jax.random.normal(k3, (INTER,), dtype=jnp.float32) * 0.02
        W2 = jax.random.normal(k4, (INTER, HIDDEN), dtype=jnp.float32) * (1.0 / np.sqrt(INTER))
        b2 = jax.random.normal(k5, (HIDDEN,), dtype=jnp.float32) * 0.02
        return {'hidden_states': hidden_states, 'W1': W1, 'b1': b1, 'W2': W2, 'b2': b2}
    _L0_ffn_in = _L0_ffn_setup()
    _d = {'L0_attn_x': _L0_attn_in['x'], 'L0_attn_wq1': _L0_attn_in['wq1'], 'L0_attn_bq1': _L0_attn_in['bq1'], 'L0_attn_wk1': _L0_attn_in['wk1'], 'L0_attn_bk1': _L0_attn_in['bk1'], 'L0_attn_wv1': _L0_attn_in['wv1'], 'L0_attn_bv1': _L0_attn_in['bv1'], 'L0_attn_wo1': _L0_attn_in['wo1'], 'L0_attn_bo1': _L0_attn_in['bo1'], 'L0_attn_wq2': _L0_attn_in['wq2'], 'L0_attn_bq2': _L0_attn_in['bq2'], 'L0_attn_wk2': _L0_attn_in['wk2'], 'L0_attn_bk2': _L0_attn_in['bk2'], 'L0_attn_wv2': _L0_attn_in['wv2'], 'L0_attn_bv2': _L0_attn_in['bv2'], 'L0_attn_wo2': _L0_attn_in['wo2'], 'L0_attn_bo2': _L0_attn_in['bo2'], 'L0_attn_g1': _L0_attn_in['g1'], 'L0_attn_be1': _L0_attn_in['be1'], 'L0_attn_g2': _L0_attn_in['g2'], 'L0_attn_be2': _L0_attn_in['be2'], 'L0_attn_w_ff1': _L0_attn_in['w_ff1'], 'L0_attn_b_ff1': _L0_attn_in['b_ff1'], 'L0_attn_w_ff2': _L0_attn_in['w_ff2'], 'L0_attn_b_ff2': _L0_attn_in['b_ff2'], 'L0_attn_g_ff': _L0_attn_in['g_ff'], 'L0_attn_be_ff': _L0_attn_in['be_ff'], 'L0_ffn_W1': _L0_ffn_in['W1'], 'L0_ffn_b1': _L0_ffn_in['b1'], 'L0_ffn_W2': _L0_ffn_in['W2'], 'L0_ffn_b2': _L0_ffn_in['b2']}
    _x0 = _d['L0_attn_x']
    _d['L0_attn_x'] = jax.random.normal(jax.random.fold_in(jax.random.key(seed), 1), (4, 2048, 256), dtype=_x0.dtype)
    del _x0
    return _d

def reference(L0_attn_x, L0_attn_wq1, L0_attn_bq1, L0_attn_wk1, L0_attn_bk1, L0_attn_wv1, L0_attn_bv1, L0_attn_wo1, L0_attn_bo1, L0_attn_wq2, L0_attn_bq2, L0_attn_wk2, L0_attn_bk2, L0_attn_wv2, L0_attn_bv2, L0_attn_wo2, L0_attn_bo2, L0_attn_g1, L0_attn_be1, L0_attn_g2, L0_attn_be2, L0_attn_w_ff1, L0_attn_b_ff1, L0_attn_w_ff2, L0_attn_b_ff2, L0_attn_g_ff, L0_attn_be_ff, L0_ffn_W1, L0_ffn_b1, L0_ffn_W2, L0_ffn_b2):

    def _L0_attn_ref(x, wq1, bq1, wk1, bk1, wv1, bv1, wo1, bo1, wq2, bq2, wk2, bk2, wv2, bv2, wo2, bo2, g1, be1, g2, be2, w_ff1, b_ff1, w_ff2, b_ff2, g_ff, be_ff):
        import jax, jax.numpy as jnp
        import numpy as np
        from jax import lax
        B, S, D = (8, 256, 256)
        DH = D // 2
        H = 8
        DK = DH // H
        DFF = 4 * D
        ALPHA, BETA = (0.1, 0.1)
        EPS = 1e-05
        PARAM_SPECS = [('wq1', (DH, DH)), ('bq1', (DH,)), ('wk1', (DH, DH)), ('bk1', (DH,)), ('wv1', (DH, DH)), ('bv1', (DH,)), ('wo1', (DH, DH)), ('bo1', (DH,)), ('wq2', (DH, DH)), ('bq2', (DH,)), ('wk2', (DH, DH)), ('bk2', (DH,)), ('wv2', (DH, DH)), ('bv2', (DH,)), ('wo2', (DH, DH)), ('bo2', (DH,)), ('g1', (DH,)), ('be1', (DH,)), ('g2', (DH,)), ('be2', (DH,)), ('w_ff1', (DFF, D)), ('b_ff1', (DFF,)), ('w_ff2', (D, DFF)), ('b_ff2', (D,)), ('g_ff', (D,)), ('be_ff', (D,))]

        def layernorm(x, g, b):
            m = jnp.mean(x, axis=-1, keepdims=True)
            v = jnp.mean(jnp.square(x - m), axis=-1, keepdims=True)
            return (x - m) * lax.rsqrt(v + EPS) * g + b

        def mha(xin, wq, bq, wk, bk, wv, bv, wo, bo):
            b, s, _ = xin.shape
            q = (xin @ wq.T + bq).reshape(b, s, H, DK)
            k = (xin @ wk.T + bk).reshape(b, s, H, DK)
            v = (xin @ wv.T + bv).reshape(b, s, H, DK)
            scores = jnp.einsum('bshd,bthd->bhst', q, k) * (1.0 / np.sqrt(DK).astype(np.float32))
            a = jax.nn.softmax(scores, axis=-1)
            o = jnp.einsum('bhst,bthd->bshd', a, v).reshape(b, s, DH)
            return o @ wo.T + bo

        def holt(x, alpha, beta):
            x0 = x[:, 0]

            def step(carry, xt):
                level, trend = carry
                nl = alpha * xt + (1.0 - alpha) * (level + trend)
                nt = beta * (nl - level) + (1.0 - beta) * trend
                return ((nl, nt), nl)
            _, lv = lax.scan(step, (x0, jnp.zeros_like(x0)), jnp.swapaxes(x[:, 1:], 0, 1))
            return jnp.concatenate([x0[:, None], jnp.swapaxes(lv, 0, 1)], axis=1)
        xh = x[:, :, :DH]
        x1 = layernorm(xh + mha(xh, wq1, bq1, wk1, bk1, wv1, bv1, wo1, bo1), g1, be1)
        xs = holt(x, ALPHA, BETA)
        xsh = xs[:, :, :DH]
        x2 = layernorm(xsh + mha(xsh, wq2, bq2, wk2, bk2, wv2, bv2, wo2, bo2), g2, be2)
        y = jnp.concatenate([x1, x2], axis=-1)
        y_ff = jax.nn.relu(y @ w_ff1.T + b_ff1) @ w_ff2.T + b_ff2
        return layernorm(y + y_ff, g_ff, be_ff)

    def _L0_ffn_ref(hidden_states, W1, b1, W2, b2):
        import jax, jax.numpy as jnp
        import numpy as np
        HIDDEN = 256
        INTER = 1024
        h = jax.nn.relu(jnp.einsum('bsh,hi->bsi', hidden_states, W1) + b1)
        return jnp.einsum('bsi,ih->bsh', h, W2) + b2
    x = L0_attn_x
    xn = _layernorm(x, axis=-1)
    x = x + _L0_attn_ref(xn, L0_attn_wq1, L0_attn_bq1, L0_attn_wk1, L0_attn_bk1, L0_attn_wv1, L0_attn_bv1, L0_attn_wo1, L0_attn_bo1, L0_attn_wq2, L0_attn_bq2, L0_attn_wk2, L0_attn_bk2, L0_attn_wv2, L0_attn_bv2, L0_attn_wo2, L0_attn_bo2, L0_attn_g1, L0_attn_be1, L0_attn_g2, L0_attn_be2, L0_attn_w_ff1, L0_attn_b_ff1, L0_attn_w_ff2, L0_attn_b_ff2, L0_attn_g_ff, L0_attn_be_ff) + _L0_ffn_ref(xn, L0_ffn_W1, L0_ffn_b1, L0_ffn_W2, L0_ffn_b2)
    return x

_drawn_inputs = setup_inputs


def setup_inputs(seed=0):
    import zlib

    import numpy as np

    out = dict(_drawn_inputs(seed))
    spreads = {'L0_attn_bq1': (0.0, 0.8),
     'L0_attn_bk1': (0.0, 2.0),
     'L0_attn_bv1': (0.0, 0.8),
     'L0_attn_bo1': (0.0, 0.307),
     'L0_attn_bq2': (0.0, 2.0),
     'L0_attn_bk2': (0.0, 2.0),
     'L0_attn_bv2': (0.0, 0.319),
     'L0_attn_bo2': (0.0, 0.1),
     'L0_attn_g1': (1.0, 0.2),
     'L0_attn_be1': (0.0, 0.1),
     'L0_attn_g2': (1.0, 0.2),
     'L0_attn_be2': (0.0, 0.1),
     'L0_attn_b_ff1': (0.0, 0.336),
     'L0_attn_b_ff2': (0.0, 0.1),
     'L0_attn_g_ff': (1.0, 0.2),
     'L0_attn_be_ff': (0.0, 0.1)}
    factors = {'L0_attn_wq1': 8.0,
     'L0_attn_wk1': 8.0,
     'L0_attn_wv1': 8.0,
     'L0_attn_wo1': 6.206,
     'L0_attn_wq2': 29.226,
     'L0_attn_wk2': 24.689,
     'L0_attn_wv2': 8.0,
     'L0_ffn_b1': 7.667,
     'L0_ffn_b2': 5.504}
    for name, (base, spread) in spreads.items():
        noise = np.random.default_rng([zlib.crc32(name.encode()), seed]).standard_normal(out[name].shape)
        drawn = base * np.exp(spread * noise) if base else spread * noise
        out[name] = jnp.asarray(drawn.astype(out[name].dtype))
    for name, factor in factors.items():
        out[name] = (out[name] * factor).astype(out[name].dtype)
    return out
```

```python
import numpy as np
import concourse.bass as bass
from concourse import mybir
from contextlib import ExitStack, contextmanager

B, S, D = 4, 2048, 256
DH = D // 2
HEADS, DK = 8, 16
FF = 1024
EPS = 1e-5
ALPHA, BETA = 0.1, 0.1
P = 128
TILES = S // P
CHUNK = 512
CHUNKS = S // CHUNK
CT = CHUNK // P
GROUPS = 2
GH = HEADS // GROUPS
ROW = P // GH
HB = FF // P
SLOT = 1024
SLOTS = 4

K_PART = [0, 1, 0, 2, 0, 1]
Q_PART = [0, 0, 1, 0, 2, 1]
STACK = DK * len(K_PART)
ROWS = STACK + 2

_WIDTHS = [("wqk", 4 * P), ("bqk", 4), ("wv", 2 * HEADS * ROW), ("bv", 2 * HEADS * ROW), ("wo", 2 * GROUPS * P),
           ("bo", 2 * DH), ("gamma", D), ("beta", D), ("gamma_ff", D), ("beta_ff", D), ("b_ff2", D), ("b2", D),
           ("b_ff1", HB), ("b1", HB), ("ident", P), ("holt", CHUNK), ("holt_state", 2 * CT), ("carry", CHUNK),
           ("carry_state", 2)]
COLS, _at = {}, 0
for _name, _w in _WIDTHS:
    COLS[_name] = (_at, _at + _w)
    _at += _w
N_COLS = _at

PRE_USES = 8
MAX_USES = {"sample": 4, "all": HEADS * TILES * 2}
SAMPLE = 32
UNITS = GROUPS * CHUNKS
STEPS = 2 * TILES


class Steps:

    def __init__(self, eng, sem):
        self.eng, self.sem, self.base, self.n = eng, sem, 0, 0

    def __call__(self, instruction):
        self.n += 1
        return instruction.then_inc(self.sem, 1)

    def settle(self, wait=None):
        (wait or self.eng.wait_ge)(*(() if wait is None else (self.eng,)), self.sem, self.base + self.n)

    @contextmanager
    def over(self, times, per):
        base, n = self.base, self.n
        with self.eng.Fori(0, times) as i:
            self.base = base + i * per
            yield i
            assert self.n == n + per, (self.n - n, per)
        self.base, self.n = base, n + times * per


def build(nc, x, packed, w_ff, w_ffn, out, mode="all"):
    f32, bf16, i32 = mybir.dt.float32, mybir.dt.bfloat16, mybir.dt.int32
    ALU, ACT, AX = mybir.AluOpType, mybir.ActivationFunctionType, mybir.AxisListType
    ds = bass.ds
    branch_uses = 8 + MAX_USES[mode] + 1 + 2
    uses = PRE_USES + 2 * branch_uses

    ctx = ExitStack()
    with ctx:
        def sb(name, shape, dt=f32):
            return ctx.enter_context(nc.sbuf_tensor(name, shape, dt))

        def sem(name):
            return ctx.enter_context(nc.semaphore(name))

        con = sb("con", [P, N_COLS])
        xn = sb("xn", [P, TILES, D])
        xt = sb("xt", [P, 2, S])
        xt_hi = sb("xt_hi", [P, S])
        shared = sb("shared", [P, GROUPS, S])
        k_st = sb("k_st", [P, HEADS, S], bf16)
        q_st = sb("q_st", [P, HEADS, S], bf16)
        v_sb = sb("v_sb", [P, TILES, HEADS, ROW])
        p_sb = sb("p_sb", [P, 4, SLOT])
        w2_sb = sb("w2_sb", [P, 4 * SLOT])
        negmax = sb("negmax", [P, P])
        halfmax = sb("halfmax", [P, P, 2])
        negmax_t = sb("negmax_t", [P, 2, P], bf16)
        state = sb("state", [2, CHUNKS, DH])
        den = sb("den", [P, CHUNK])
        rden = sb("rden", [P, CHUNK])
        stats = sb("stats", [P, TILES, 6])
        mv = sb("mv", [P, TILES, 2])
        rs = sb("rs", [P, 4, TILES])
        m_dram = nc.dram_tensor("m_dram", (2, P, P), bf16, kind="Internal").ap()

        def c(name):
            return con[:, COLS[name][0]:COLS[name][1]]

        wqk = c("wqk").rearrange("p (i n) -> p i n", i=4)
        bqk = c("bqk")
        wv = c("wv").rearrange("p (a n) -> p a n", a=2)
        bv = c("bv").rearrange("p (a n) -> p a n", a=2)
        wo = c("wo").rearrange("p (a g n) -> p a g n", a=2, g=GROUPS)
        bo = c("bo").rearrange("p (a n) -> p a n", a=2)
        ident = c("ident")
        holt = c("holt")
        holt_state = c("holt_state").rearrange("p (j i) -> p j i", i=2)
        carry = c("carry")[0:2, :]
        carry_state = c("carry_state")[0:2, :]
        parts = shared[:, :, :].rearrange("p g s -> p (g s)").bitcast(bf16)[:, 0:3 * S].rearrange("p (i s) -> p i s", i=3)
        rest = shared[:, :, :].rearrange("p g s -> p (g s)")[:, 3 * SLOT:4 * SLOT]
        hidden = p_sb[:, :, :].rearrange("p i n -> p (i n)").rearrange("p (m n) -> p m n", m=HB)
        w_ff_flat = v_sb[:, :, :, :].rearrange("p t h n -> p (t h n)")

        def net(flat):
            return (flat[:, 0:2 * FF].rearrange("p (k n) -> p k n", k=2),
                    flat[:, 2 * FF:4 * FF].rearrange("p (m n) -> p m n", m=HB))

        ff1, ff2 = net(w_ff_flat)
        fn1, fn2 = net(w2_sb[:, :])
        tail = q_st[:, :, :].rearrange("p h s -> p (h s)").bitcast(f32)
        y_sb, yt_sb, x_raw, o_sb = (tail[:, i * SLOT:(i + 1) * SLOT] for i in range(4))
        y4 = y_sb.rearrange("p (t n) -> p t n", t=CT)
        yt2 = yt_sb.rearrange("p (k n) -> p k n", k=2)
        x4 = x_raw.rearrange("p (t n) -> p t n", t=CT)
        o4 = o_sb.rearrange("p (t n) -> p t n", t=CT)

        slot = [ctx.enter_context(nc.psum_tensor(f"slot{i}", [P, SLOT], f32)) for i in range(SLOTS)]
        o_bank = [slot[3][:, i * CHUNK:(i + 1) * CHUNK] for i in range(2)]

        consts_in = sem("consts_in")
        x_in = sem("x_in")
        ff_in = sem("ff_in")
        xn_ready = sem("xn_ready")
        work_made = sem("work_made")
        work_read = sem("work_read")
        state_saved = sem("state_saved")
        state_made = sem("state_made")
        biased = sem("biased")
        first_part = sem("first_part")
        parts_ready = sem("parts_ready")
        k_in = sem("k_in")
        q_in = sem("q_in")
        negmax_ready = sem("negmax_ready")
        negmax_parts = sem("negmax_parts")
        m_out = sem("m_out")
        m_in = sem("m_in")
        scores_made = sem("scores_made")
        exp_done = sem("exp_done")
        pv_done = sem("pv_done")
        o_read = sem("o_read")
        resid_ready = sem("resid_ready")
        hid_made = sem("hid_made")
        hid_read = sem("hid_read")
        ffn_made = sem("ffn_made")
        ffn_read = sem("ffn_read")
        y_ready = sem("y_ready")
        yt_made = sem("yt_made")
        yt_saved = sem("yt_saved")
        ff_made = sem("ff_made")
        ff_read = sem("ff_read")
        xr_in = sem("xr_in")
        o_ready = sem("o_ready")
        stored = sem("stored")
        ones_set = sem("ones_set")
        dve_steps = sem("dve_steps")
        held = sem("held")

        def hold(eng, semaphore, value):
            eng.wait_ge(semaphore, value)
            eng.sem_inc(held, 1)

        block = ctx.enter_context(nc.Block())

        x_v = x.rearrange("b (t p) d -> b p t d", p=P)
        out_v = out.rearrange("b (t p) d -> b p t d", p=P)

        @block.sync
        def _(sp):
            sp.dma_start(con[:, :], packed).then_inc(consts_in, 16)
            sp.dma_start(w2_sb[:, :], w_ffn).then_inc(consts_in, 16)
            with sp.Fori(0, B) as b:
                sp.wait_ge(y_ready, b * CHUNKS)
                for i in range(CHUNKS):
                    sp.dma_start(xn[:, i * CT:(i + 1) * CT, :],
                                 x_v[ds(b, 1), :, i * CT:(i + 1) * CT, :].rearrange("b p t d -> p (b t) d")).then_inc(x_in, 16)
                for a in range(2):
                    p_ = 2 * b + a
                    for which, (stack, order, done) in enumerate(((k_st, K_PART, k_in), (q_st, Q_PART, q_in))):
                        hold(sp, parts_ready, 4 * p_ + 2 * which + 2)
                        if which == 1 and a == 0:
                            hold(sp, stored, 16 * CHUNKS * b)
                        for r, part in enumerate(order):
                            for h in range(HEADS):
                                sp.dma_start(stack[DK * r:DK * (r + 1), h, :],
                                             parts[DK * h:DK * (h + 1), part, :]).then_inc(done, 16)
                    sp.wait_ge(negmax_parts, p_ + 1)
                    sp.dma_start(m_dram.rearrange("i p n -> p i n"), negmax_t[:, :, :]).then_inc(m_out, 16)
                    sp.wait_ge(m_out, 16 * (p_ + 1))
                    sp.dma_start(q_st[STACK:ROWS, :, :].rearrange("i h s -> i (h s)"),
                                 m_dram.rearrange("i p n -> i (p n)")).then_inc(m_in, 16)
                sp.wait_ge(work_made, (b + 1) * uses)
                sp.dma_start(w_ff_flat, w_ff).then_inc(ff_in, 16)
                with sp.Fori(0, CHUNKS) as cc:
                    n = CHUNKS * b + cc
                    sp.wait_ge(o_ready, n)
                    sp.dma_start(x4, x_v[ds(b, 1), :, ds(cc * CT, CT), :].rearrange("b p t d -> p (b t) d")).then_inc(xr_in, 16)
                    sp.wait_ge(o_ready, n + 1)
                    sp.dma_start(out_v[ds(b, 1), :, ds(cc * CT, CT), :].rearrange("b p t d -> p (b t) d"), o4).then_inc(stored, 16)
            sp.wait_ge(stored, 16 * CHUNKS * B)

        @block.gpsimd
        def _(pool):
            pool.memset(k_st[STACK:P, :, :], 1.0).then_inc(ones_set, 1)
            with pool.Fori(0, B) as b:
                pool.wait_ge(work_made, b * uses + 6)
                pool.wait_ge(consts_in, 32)
                pool.tensor_tensor(xn[:, :, 0:DH], xn[:, :, 0:DH],
                                   bo[:, 0:1, :].broadcast_to([P, TILES, DH]), ALU.add).then_inc(biased, 1)

        @block.scalar
        def _(act):
            act.sem_inc(exp_done, 3)
            act.sem_inc(hid_read, 4)
            act.wait_ge(consts_in, 32)
            with act.Fori(0, B) as b:
                for a in range(2):
                    p_ = 2 * b + a
                    j0 = b * uses + PRE_USES + a * branch_uses
                    for which, first in ((0, 0), (1, 6)):
                        for i in range(2):
                            act.wait_ge(work_made, j0 + first + i + 1)
                            if which == 1:
                                act.wait_ge(k_in, 16 * HEADS * 6 * (p_ + 1))
                            act.activation(parts[:, 0, i * SLOT:(i + 1) * SLOT], slot[(first + i) % SLOTS][:, :], ACT.Identity,
                                           bias=bqk[:, 2 * a + which:2 * a + which + 1]).then_inc(first_part, 1)
                    for g in range(GROUPS):
                        with act.Fori(0, CHUNKS // 2) as cp:
                            for i in range(2):
                                u = UNITS * p_ + CHUNKS * g + 2 * cp + i
                                for s in range(STEPS):
                                    act.wait_ge(scores_made, STEPS * u + s + 1)
                                    if s % 2 == 0:
                                        act.wait_ge(pv_done, TILES * u + s // 2 + 1)
                                    act.activation(p_sb[:, s % 4, :], slot[s % 3][:, :], ACT.Exp, scale=0.25).then_inc(exp_done, 1)
                with act.Fori(0, CHUNKS) as cc:
                    n = CHUNKS * b + cc
                    for which, bias in enumerate((c("b1"), c("b_ff1"))):
                        if which == 0:
                            act.wait_ge(ff_made, n)
                        else:
                            act.wait_ge(ffn_made, n + 1)
                        for m in range(HB):
                            act.wait_ge(hid_made, 2 * HB * n + HB * which + m + 1)
                            act.activation(hidden[:, m, :], slot[m // 2 % 2][:, (m % 2) * CHUNK:(m % 2 + 1) * CHUNK], ACT.Relu,
                                           bias=bias[:, m:m + 1]).then_inc(hid_read, 1)

        @block.vector
        def _(dve):
            step = Steps(dve, dve_steps)
            dve.sem_inc(work_read, SLOTS)
            dve.sem_inc(o_read, 2)
            dve.wait_ge(consts_in, 32)

            def rsqrt(n):
                v, r, t = rs[:, 0, 0:n], rs[:, 1, 0:n], rs[:, 2, 0:n]
                step(dve.tensor_scalar(v, mv[:, 0:n, 1], EPS, None, ALU.add))
                step.settle()
                step(dve.tensor_scalar(t.bitcast(i32), v.bitcast(i32), 1, None, ALU.logical_shift_right))
                step.settle()
                step(dve.tensor_scalar(r.bitcast(i32), t.bitcast(i32), -1.0, float(0x5F3759DF), ALU.mult, ALU.add))
                for _ in range(4):
                    step.settle()
                    step(dve.tensor_tensor(t, r, r, ALU.mult))
                    step.settle()
                    step(dve.scalar_tensor_tensor(t, t, -0.5, v, ALU.mult, ALU.mult))
                    step.settle()
                    step(dve.scalar_tensor_tensor(r, t, 1.5, r, ALU.add, ALU.mult))
                step.settle()

            def normalise(srcs, dsts):
                for i, s in enumerate(srcs):
                    step(dve.bn_stats(stats[:, i, :], s))
                step.settle(hold)
                for i in range(len(srcs)):
                    step(dve.bn_aggr(mv[:, i, :], stats[:, i, :]))
                step.settle()
                rsqrt(len(srcs))
                for i, (s, d) in enumerate(zip(srcs, dsts)):
                    ins = step(dve.tensor_scalar(d, s, mv[:, i, 0:1], rs[:, 1, i:i + 1], ALU.subtract, ALU.mult))
                return ins

            def rows(name, k):
                lo, hi = COLS[name]
                return con[:, lo:hi].rearrange("p (k n) -> p k n", k=1).broadcast_to([P, k, hi - lo])

            step(dve.tensor_tensor(c("b2"), c("b2"), c("beta_ff"), ALU.add))
            step.settle()
            N_RS = 3 + 12
            PER_UNIT = 2
            per_pair = 2 * PER_UNIT
            per_chunk = (8 + 8 + N_RS + 8) + 1 + 1 + (4 + 4 + N_RS + 4) + 2
            per_branch = 2 * 2 + 1 + GROUPS * (CHUNKS // 2) * per_pair
            per_batch = (16 + 16 + N_RS + 16) + 2 * per_branch + CHUNKS * per_chunk
            with step.over(B, per_batch) as b:
                w0 = b * uses
                dve.wait_ge(x_in, 64 * (b + 1))
                tiles = [xn[:, t, :] for t in range(TILES)]
                normalise(tiles, tiles)
                step.settle()
                dve.memset(state[:, :, :], 0.0).then_inc(xn_ready, 1)
                dve.wait_ge(xn_ready, b + 1)
                dve.tensor_copy(state[0:1, 0, :], xn[0:1, 0, 0:DH]).then_inc(state_saved, 1)
                for j in range(4):
                    dve.wait_ge(work_made, w0 + j + 1)
                    dst = (xt[:, 0, :] if j < 2 else xt_hi[:, :])[:, (j % 2) * SLOT:(j % 2 + 1) * SLOT]
                    dve.tensor_copy(dst, slot[j][:, :]).then_inc(work_read, 1)
                for k in range(1, CHUNKS):
                    dve.wait_ge(state_made, (CHUNKS - 1) * b + k)
                    dve.tensor_copy(state[:, k, :], slot[3][0:2, k * P:(k + 1) * P]).then_inc(state_saved, 1)
                for j in range(4, 6):
                    dve.wait_ge(work_made, w0 + j + 1)
                    dve.tensor_copy(xt[:, 1, (j % 2) * SLOT:(j % 2 + 1) * SLOT], slot[j - 4][:, :]).then_inc(work_read, 1)
                for j in range(6, 8):
                    dve.wait_ge(work_made, w0 + j + 1)
                    dve.tensor_tensor(xn[:, (j % 2) * 8:(j % 2 + 1) * 8, DH:D], slot[j - 4][:, :].rearrange("p (t n) -> p t n", t=8),
                                      bo[:, 1:2, :].broadcast_to([P, 8, DH]), ALU.add).then_inc(work_read, 1)
                for a in range(2):
                    p_ = 2 * b + a
                    j0 = w0 + PRE_USES + a * branch_uses

                    def split(which, first):
                        bias = bqk[:, 2 * a + which:2 * a + which + 1]
                        for i in range(2):
                            lo, hi = i * SLOT, (i + 1) * SLOT
                            dve.wait_ge(first_part, 4 * p_ + 2 * which + i + 1)
                            dve.scalar_tensor_tensor(rest, slot[(first + i) % SLOTS][:, :], bias, parts[:, 0, lo:hi],
                                                     ALU.add, ALU.subtract).then_inc(work_read, 1)
                            dve.wait_ge(work_read, j0 + first + i + 1 + SLOTS)
                            step(dve.tensor_copy(parts[:, 1, lo:hi], rest))
                            step.settle()
                            dve.tensor_tensor(parts[:, 2, lo:hi], rest, parts[:, 1, lo:hi], ALU.subtract).then_inc(parts_ready, 1)
                            hold(dve, parts_ready, 4 * p_ + 2 * which + i + 1)

                    split(0, 0)
                    for j in range(2, 6):
                        dve.wait_ge(work_made, j0 + j + 1)
                        dve.tensor_tensor(v_sb[:, (j - 2) * 4:(j - 1) * 4, :, :].rearrange("p t h n -> p t (h n)"),
                                          slot[j % SLOTS][:, :].rearrange("p (t n) -> p t n", t=4),
                                          bv[:, a:a + 1, :].broadcast_to([P, 4, HEADS * ROW]), ALU.add).then_inc(work_read, 1)
                    split(1, 6)
                    if mode == "all":
                        with dve.Fori(0, TILES) as qt:
                            for i in range(2 * HEADS):
                                dve.wait_ge(work_made, j0 + 8 + 2 * HEADS * qt + i + 1)
                                dve.reduce_max(halfmax[:, ds((i // 2) * TILES + qt, 1), i % 2], slot[i % SLOTS][:, :], AX.X)\
                                   .then_inc(work_read, 1)
                        dve.wait_ge(work_read, j0 + 8 + MAX_USES[mode] + SLOTS)
                        dve.tensor_reduce(negmax[:, :], halfmax[:, :, :], AX.X, ALU.max, negate=True).then_inc(negmax_ready, 1)
                    else:
                        for i in range(4):
                            dve.wait_ge(work_made, j0 + 8 + i + 1)
                            dve.tensor_reduce(negmax[:, i * 32:(i + 1) * 32], slot[i][:, :].rearrange("p (m k) -> p m k", k=SAMPLE),
                                              AX.X, ALU.max, negate=True).then_inc(work_read, 1)
                    dve.wait_ge(work_made, j0 + 8 + MAX_USES[mode] + 1)
                    step(dve.tensor_copy(negmax_t[:, 0, :], slot[0][:, 0:P]))
                    step.settle()
                    dve.tensor_tensor(negmax_t[:, 1, :], slot[0][:, 0:P], negmax_t[:, 0, :], ALU.subtract).then_inc(negmax_parts, 1)
                    dve.wait_ge(negmax_parts, p_ + 1)
                    dve.sem_inc(work_read, 1)
                    for g in range(GROUPS):
                        with step.over(CHUNKS // 2, per_pair) as cp:
                            for i in range(2):
                                u = UNITS * p_ + CHUNKS * g + 2 * cp + i
                                hold(dve, pv_done, TILES * (u + 1) + 2)
                                step(dve.stream_shuffle(den[:, :], o_bank[i], [DK] * 32))
                                step.settle()
                                step(dve.reciprocal(rden[:, :], den[:, :]))
                                step.settle()
                                dve.tensor_tensor(shared[:, g, ds((2 * cp + i) * CHUNK, CHUNK)], o_bank[i], rden[:, :], ALU.mult)\
                                   .then_inc(o_read, 1)
                    if a == 0:
                        dve.wait_ge(biased, b + 1)
                    for i in range(2):
                        dve.wait_ge(work_made, j0 + branch_uses - 2 + i + 1)
                        half = xn[:, 8 * i:8 * (i + 1), a * DH:(a + 1) * DH]
                        dve.tensor_tensor(half, slot[i][:, :].rearrange("p (t n) -> p t n", t=8), half, ALU.add)\
                           .then_inc(work_read, 1)
                hold(dve, work_read, (b + 1) * uses + SLOTS)
                with step.over(CHUNKS, per_chunk) as cc:
                    n = CHUNKS * b + cc
                    srcs = [xn[:, ds(cc * CT + t, 1), a * DH:(a + 1) * DH].rearrange("p t n -> p (t n)")
                            for t in range(CT) for a in range(2)]
                    normalise(srcs, [y4[:, t, a * DH:(a + 1) * DH] for t in range(CT) for a in range(2)])
                    step.settle()
                    step(dve.tensor_tensor(y4, y4, rows("gamma", CT), ALU.mult))
                    step.settle()
                    dve.tensor_tensor(y4, y4, rows("beta", CT), ALU.add).then_inc(y_ready, 1)
                    dve.wait_ge(y_ready, n + 1)
                    dve.wait_ge(yt_made, n + 1)
                    dve.tensor_copy(yt_sb, slot[2][:, :]).then_inc(yt_saved, 1)
                    dve.wait_ge(ff_made, n + 1)
                    dve.wait_ge(stored, 16 * n)
                    dve.tensor_tensor(o4, slot[2][:, :].rearrange("p (t n) -> p t n", t=CT), y4, ALU.add).then_inc(ff_read, 1)
                    dve.wait_ge(ff_read, n + 1)
                    step(dve.tensor_tensor(o4, o4, rows("b_ff2", CT), ALU.add))
                    step.settle()
                    tiles = [o4[:, t, :] for t in range(CT)]
                    normalise(tiles, tiles)
                    step.settle()
                    step(dve.tensor_tensor(o4, o4, rows("gamma_ff", CT), ALU.mult))
                    step.settle()
                    dve.tensor_tensor(o4, slot[3][:, :].rearrange("p (t n) -> p t n", t=CT), o4, ALU.add).then_inc(ffn_read, 1)
                    dve.wait_ge(ffn_read, n + 1)
                    step(dve.tensor_tensor(o4, o4, rows("b2", CT), ALU.add))
                    step.settle()
                    dve.wait_ge(xr_in, 16 * (n + 1))
                    dve.tensor_tensor(o4, o4, x4, ALU.add).then_inc(o_ready, 1)

        @block.tensor
        def _(pe):
            pe.sem_inc(pv_done, 2)
            pe.wait_ge(consts_in, 32)
            pe.wait_ge(ones_set, 1)
            with pe.Fori(0, B) as b:
                w0 = b * uses

                def free(j, whole=False):
                    pe.wait_ge(work_read, w0 + j + (SLOTS if whole else 1))

                def transpose8(sl, src, at):
                    for t in range(8):
                        mm = pe.transpose(sl[:, t * P:(t + 1) * P], src(8 * at + t), ident)
                    mm.then_inc(work_made, 1)

                free(0, True)
                pe.wait_ge(xn_ready, b + 1)
                pe.wait_ge(ffn_read, CHUNKS * b)
                pe.wait_ge(ff_read, CHUNKS * b)
                pe.wait_ge(hid_read, 2 * HB * CHUNKS * b + 4)
                for j in range(4):
                    transpose8(slot[j], lambda t: xn[:, t, (j // 2) * DH:(j // 2 + 1) * DH], j % 2)
                pe.wait_ge(work_read, w0 + 4 + SLOTS)
                for k in range(CHUNKS):
                    bank = slot[k // 2][:, (k % 2) * CHUNK:(k % 2 + 1) * CHUNK]
                    hold(pe, state_saved, CHUNKS * b + k + 1)
                    if k + 1 < CHUNKS:
                        after = slot[3][0:2, (k + 1) * P:(k + 2) * P]
                        pe.matmul(after, carry_state, state[:, k, :], start=True, stop=False)
                        for t in range(CT):
                            mm = pe.matmul(after, holt_state[:, t, :], xn[:, CT * k + t, 0:DH], start=False, stop=(t == CT - 1))
                        mm.then_inc(state_made, 1)
                    pe.matmul(bank, state[:, k, :], carry, start=True, stop=False)
                    for t in range(CT):
                        mm = pe.matmul(bank[:, t * P:], xn[:, CT * k + t, 0:DH], holt[:, 0:CHUNK - t * P],
                                       start=False, stop=(t == CT - 1))
                    if k % 2:
                        mm.then_inc(work_made, 1)
                for j in range(6, 8):
                    pe.wait_ge(work_read, w0 + 6 + SLOTS)
                    transpose8(slot[j - 4], lambda t: xt[:, 1, t * P:(t + 1) * P], j % 2)
                for a in range(2):
                    p_ = 2 * b + a
                    jb = PRE_USES + a * branch_uses

                    def project(which, first):
                        for i in range(2):
                            free(jb + first + i)
                            for k in range(2):
                                mm = pe.matmul(slot[(first + i) % SLOTS][:, k * CHUNK:(k + 1) * CHUNK], wqk[:, 2 * a + which, :],
                                               xt[:, a, (2 * i + k) * CHUNK:(2 * i + k + 1) * CHUNK], start=True, stop=True)
                            mm.then_inc(work_made, 1)

                    free(jb, True)
                    project(0, 0)
                    for j in range(2, 6):
                        free(jb + j)
                        for t in range(4):
                            tok = (j - 2) * 4 + t
                            mm = pe.matmul(slot[j % SLOTS][:, t * D:(t + 1) * D], xt[:, a, tok * P:(tok + 1) * P], wv[:, a, :],
                                           start=True, stop=True)
                        mm.then_inc(work_made, 1)
                    project(1, 6)
                    pe.wait_ge(k_in, 16 * HEADS * 6 * (p_ + 1))
                    hold(pe, q_in, 16 * HEADS * 6 * (p_ + 1))
                    if mode == "all":
                        with pe.Fori(0, TILES) as qt:
                            for i in range(2 * HEADS):
                                free(jb + 8 + 2 * HEADS * qt + i)
                                h = i // 2
                                for k in range(2):
                                    at = (2 * (i % 2) + k) * CHUNK
                                    mm = pe.matmul(slot[i % SLOTS][:, k * CHUNK:(k + 1) * CHUNK], q_st[0:STACK, h, ds(qt * P, P)],
                                                   k_st[0:STACK, h, at:at + CHUNK], start=True, stop=True)
                                mm.then_inc(work_made, 1)
                    else:
                        for i in range(4):
                            free(jb + 8 + i)
                            for m in range(2 * TILES):
                                h, qt = 2 * i + m // TILES, m % TILES
                                mm = pe.matmul(slot[i][:, m * SAMPLE:(m + 1) * SAMPLE], q_st[0:STACK, h, qt * P:(qt + 1) * P],
                                               k_st[0:STACK, h, 0:S:S // SAMPLE], start=True, stop=True)
                            mm.then_inc(work_made, 1)
                    jm = jb + 8 + MAX_USES[mode]
                    free(jm, True)
                    if mode == "all":
                        pe.wait_ge(negmax_ready, p_ + 1)
                    pe.transpose(slot[0][:, 0:P], negmax[:, :], ident).then_inc(work_made, 1)
                    free(jm + 1, True)
                    hold(pe, m_in, 16 * (p_ + 1))
                    for g in range(GROUPS):
                        with pe.Fori(0, CHUNKS // 2) as cp:
                            for i in range(2):
                                u = UNITS * p_ + CHUNKS * g + 2 * cp + i

                                def scores(kt):
                                    for s in (2 * kt, 2 * kt + 1):
                                        pe.wait_ge(exp_done, STEPS * u + {0: -1, 1: 0, 2: 0}.get(s, s - 2) + 3)
                                        for k in range(2):
                                            h = GH * g + 2 * (s % 2) + k
                                            mm = pe.matmul(slot[s % 3][:, k * CHUNK:(k + 1) * CHUNK], k_st[0:ROWS, h, kt * P:(kt + 1) * P],
                                                           q_st[0:ROWS, h, ds((2 * cp + i) * CHUNK, CHUNK)], start=True, stop=True)
                                        mm.then_inc(scores_made, 1)

                                scores(0)
                                for kt in range(TILES):
                                    if kt + 1 < TILES:
                                        scores(kt + 1)
                                    if kt == 0:
                                        pe.wait_ge(o_read, u + 1)
                                    pe.wait_ge(exp_done, STEPS * u + 2 * kt + 2 + 3)
                                    for j in range(GH):
                                        s = 2 * kt + j // 2
                                        mm = pe.matmul(o_bank[i][ROW * j:ROW * (j + 1), :], v_sb[:, kt, GH * g + j, :],
                                                       p_sb[:, s % 4, (j % 2) * CHUNK:(j % 2 + 1) * CHUNK],
                                                       start=(kt == 0), stop=(kt == TILES - 1), skip_group_check=True)
                                    mm.then_inc(pv_done, 1)
                    pe.wait_ge(o_read, UNITS * (p_ + 1) + 2)
                    for i in range(2):
                        for t in range(8):
                            for g in range(GROUPS):
                                tok = 8 * i + t
                                mm = pe.matmul(slot[i][:, t * P:(t + 1) * P], shared[:, g, tok * P:(tok + 1) * P], wo[:, a, g, :],
                                               start=(g == 0), stop=(g == GROUPS - 1))
                        mm.then_inc(work_made, 1)
                pe.wait_ge(work_read, w0 + uses + SLOTS)
                hold(pe, ff_in, 16 * (b + 1))
                with pe.Fori(0, CHUNKS) as cc:
                    n = CHUNKS * b + cc

                    def net_hidden(which, w1, src):
                        for m in range(HB):
                            pe.wait_ge(hid_read, 2 * HB * n + HB * which + m + 1)
                            for k in range(2):
                                mm = pe.matmul(slot[m // 2 % 2][:, (m % 2) * CHUNK:(m % 2 + 1) * CHUNK], w1[:, k, m * P:(m + 1) * P],
                                               src(k), start=(k == 0), stop=(k == 1))
                            mm.then_inc(hid_made, 1)
                        pe.wait_ge(hid_read, 2 * HB * n + HB * (which + 1) + 4)

                    def net_out(sl, w2, done):
                        for t in range(CT):
                            for m in range(HB):
                                mm = pe.matmul(sl[:, t * D:(t + 1) * D], hidden[:, m, t * P:(t + 1) * P], w2[:, m, :],
                                               start=(m == 0), stop=(m == HB - 1))
                        mm.then_inc(done, 1)

                    net_hidden(0, fn1, lambda k: (xt[:, 0, :] if k == 0 else xt_hi[:, :])[:, ds(cc * CHUNK, CHUNK)])
                    pe.wait_ge(ffn_read, n)
                    net_out(slot[3], fn2, ffn_made)
                    pe.wait_ge(y_ready, n + 1)
                    pe.wait_ge(ff_read, n)
                    for k in range(2):
                        for t in range(CT):
                            mm = pe.transpose(slot[2][:, k * CHUNK + t * P:k * CHUNK + (t + 1) * P], y4[:, t, k * P:(k + 1) * P], ident)
                    mm.then_inc(yt_made, 1)
                    pe.wait_ge(yt_saved, n + 1)
                    net_hidden(1, ff1, lambda k: yt2[:, k, :])
                    net_out(slot[2], ff2, ff_made)


def smoothing_tables():
    a = np.array([[1 - ALPHA, 1 - ALPHA], [-BETA * ALPHA, 1 - BETA * ALPHA]])
    cx = np.array([ALPHA, BETA * ALPHA])
    power = [np.eye(2)]
    for _ in range(CHUNK):
        power.append(a @ power[-1])
    hit = np.array([m @ cx for m in power])
    holt = np.zeros((P, CHUNK))
    for s in range(P):
        holt[s, s:] = hit[:CHUNK - s, 0]
    last = hit[CHUNK - 1::-1][:CHUNK].reshape(CT, P, 2).transpose(1, 0, 2)
    carry = np.array([power[t + 1][0] for t in range(CHUNK)]).T
    return holt, last.reshape(P, 2 * CT), carry, power[CHUNK].T


def kernel(**inputs):
    import concourse.bacc as bacc
    from concourse.bass_utils import run_bass_kernel_spmd

    v = {k: np.asarray(a) for k, a in inputs.items()}
    get = lambda name: v["L0_attn_" + name]
    packed = np.zeros((P, N_COLS), np.float32)

    def put(name, a):
        lo, hi = COLS[name]
        packed[:a.shape[0], lo:hi] = a.reshape(a.shape[0], hi - lo)

    def by_partition(a):
        return np.broadcast_to(a.reshape(1, -1), (P, a.size))

    put("wqk", np.stack([get(w + n).T for n in "12" for w in ("wk", "wq")], 1))
    put("bqk", np.stack([get(w + n) for n in "12" for w in ("bk", "bq")], 1))
    wv = np.zeros((P, 2, HEADS, ROW), np.float32)
    bv = np.zeros((2, HEADS, ROW), np.float32)
    bv[:, :, DK] = 1.0
    wo = np.zeros((GH, ROW, 2, GROUPS, DH), np.float32)
    for i, n in enumerate("12"):
        wv[:, i, :, :DK] = get("wv" + n).T.reshape(DH, HEADS, DK)
        bv[i, :, :DK] = get("bv" + n).reshape(HEADS, DK)
        wo[:, :DK, i] = get("wo" + n).T.reshape(GROUPS, GH, DK, DH).transpose(1, 2, 0, 3)
    put("wv", wv)
    put("bv", by_partition(bv))
    put("wo", wo.reshape(P, -1))
    put("bo", by_partition(np.concatenate([get("bo1"), get("bo2")])))
    put("gamma", by_partition(np.concatenate([get("g1"), get("g2")])))
    put("beta", by_partition(np.concatenate([get("be1"), get("be2")])))
    put("gamma_ff", by_partition(get("g_ff")))
    put("beta_ff", by_partition(get("be_ff")))
    put("b_ff2", by_partition(get("b_ff2")))
    put("b2", by_partition(v["L0_ffn_b2"]))
    put("b_ff1", get("b_ff1").reshape(HB, P).T)
    put("b1", v["L0_ffn_b1"].reshape(HB, P).T)
    put("ident", np.eye(P, dtype=np.float32))
    for name, table in zip(("holt", "holt_state", "carry", "carry_state"), smoothing_tables()):
        put(name, table)

    def net(w1, w2):
        return np.concatenate([w1.reshape(2, P, FF).transpose(1, 0, 2).reshape(P, -1),
                               w2.reshape(HB, P, D).transpose(1, 0, 2).reshape(P, -1)], 1)

    arrays = {
        "x": np.ascontiguousarray(get("x")),
        "packed": packed,
        "w_ff": net(get("w_ff1").T, get("w_ff2").T),
        "w_ffn": net(v["L0_ffn_W1"], v["L0_ffn_W2"]),
    }
    nc = bacc.Bacc("TRN2", target_bir_lowering=False, num_devices=1)
    args = [nc.dram_tensor(k, a.shape, mybir.dt.from_np(a.dtype), kind="ExternalInput").ap() for k, a in arrays.items()]
    out = nc.dram_tensor("out", (B, S, D), mybir.dt.float32, kind="ExternalOutput").ap()
    build(nc, *args, out)
    return run_bass_kernel_spmd(nc, [arrays], core_ids=[0]).results[0]["out"]
```

```python
import numpy as np
import concourse.bass as bass
from concourse import mybir
from contextlib import ExitStack, contextmanager

B, S, D = 4, 2048, 256
DH = D // 2
HEADS, DK = 8, 16
FF = 1024
EPS = 1e-5
ALPHA, BETA = 0.1, 0.1
P = 128
TILES = S // P
CHUNK = 512
CHUNKS = S // CHUNK
CT = CHUNK // P
GROUPS = 2
GH = HEADS // GROUPS
ROW = P // GH
HB = FF // P
SLOT = 1024
SUM_LIMIT = 1e30

K_PART = [0, 1, 0, 2, 0, 1]
Q_PART = [0, 0, 1, 0, 2, 1]
STACK = DK * len(K_PART)
ROWS = STACK + 2

_WIDTHS = [("wqk", 4 * P), ("bqk", 4), ("wv", 2 * HEADS * ROW), ("bv", 2 * HEADS * ROW), ("wo", 2 * GROUPS * P),
           ("bo", 2 * DH), ("gamma", D), ("beta", D), ("gamma_ff", D), ("beta_ff", D), ("b_ff2", D), ("b2", D),
           ("b_ff1", HB), ("b1", HB), ("ident", P), ("holt", CHUNK), ("holt_state", 2 * CT), ("carry", CHUNK),
           ("carry_state", 2), ("own", HEADS)]
COLS, _at = {}, 0
for _name, _w in _WIDTHS:
    COLS[_name] = (_at, _at + _w)
    _at += _w
N_COLS = _at

SAMPLE = 32
MAX_USES = {"sample": TILES * HEADS * SAMPLE // SLOT, "all": HEADS * TILES * 2}
UNITS = GROUPS * CHUNKS
STEPS = 2 * TILES
LOADS = len(K_PART) * 2 + 2


class Semaphores:

    def __init__(self, new):
        self.x_in = new("x_in")
        self.xn_ready = new("xn_ready")
        self.xn_used = new("xn_used")
        self.work_made = new("work_made")
        self.work_read = new("work_read")
        self.state_saved = new("state_saved")
        self.state_made = new("state_made")
        self.first_part = new("first_part")
        self.parts_ready = new("parts_ready")
        self.k_out = new("k_out")
        self.q_out = new("q_out")
        self.diag_ready = new("diag_ready")
        self.all_ready = new("all_ready")
        self.negmax_ready = new("negmax_ready")
        self.negmax_parts = new("negmax_parts")
        self.m_out = new("m_out")
        self.stack_in = [new(f"stack_in_{g}") for g in range(GROUPS)]
        self.scores_made = new("scores_made")
        self.exp_done = new("exp_done")
        self.pv_done = new("pv_done")
        self.o_read = new("o_read")
        self.nets_in = new("nets_in")
        self.hid_made = new("hid_made")
        self.hid_read = new("hid_read")
        self.net_done = new("net_done")
        self.second_in = new("second_in")
        self.second_ready = new("second_ready")
        self.second_out = new("second_out")
        self.y_ready = new("y_ready")
        self.yt_made = new("yt_made")
        self.yt_saved = new("yt_saved")
        self.ff_read = new("ff_read")
        self.back_in = new("back_in")
        self.o_ready = new("o_ready")
        self.stored = new("stored")
        self.step = new("dve_steps")


class Steps:

    def __init__(self, eng, sem):
        self.eng, self.sem, self.base, self.n = eng, sem, 0, 0

    def __call__(self, instruction):
        self.n += 1
        return instruction.then_inc(self.sem, 1)

    def settle(self, wait=None):
        (wait or self.eng.wait_ge)(*(() if wait is None else (self.eng,)), self.sem, self.base + self.n)

    @contextmanager
    def over(self, times, per):
        base, n = self.base, self.n
        with self.eng.Fori(0, times) as i:
            self.base = base + i * per
            yield i
            assert self.n == n + per, (self.n - n, per)
        self.base, self.n = base, n + times * per


class Order:

    def __init__(self, mode):
        self.n = 0
        self.turn = self.take(4)
        self.branch = []
        for a in range(2):
            k = self.take(2)
            state = self.take(1) if a == 0 else None
            holt = self.take(2) if a == 0 else None
            self.branch.append(dict(k=k, state=state, holt=holt, v=self.take(4), q=self.take(2),
                                    max=self.take(MAX_USES[mode]), turn=self.take(1)))
        self.resid = self.take(2)
        self.out = [self.take(2), self.take(2)]
        self.uses = self.n

    def take(self, k):
        self.n += k
        return self.n - k


def build(nc, x, packed, w_ff, w_ffn, out, modes=("sample", "all")):
    f32, bf16, i32 = mybir.dt.float32, mybir.dt.bfloat16, mybir.dt.int32
    ALU, ACT, AX = mybir.AluOpType, mybir.ActivationFunctionType, mybir.AxisListType
    ds = bass.ds

    ctx = ExitStack()
    with ctx:
        def sb(name, shape, dt=f32):
            return ctx.enter_context(nc.sbuf_tensor(name, shape, dt))

        def dram(name, shape, dt):
            return nc.dram_tensor(name, shape, dt, kind="Internal").ap()

        con = sb("con", [P, N_COLS])
        xn = sb("xn", [P, TILES, D])
        resid = sb("resid", [P, TILES, D])
        xt = sb("xt", [P, 2, S])
        xt_hi = sb("xt_hi", [P, S])
        att = xt
        v_sb = sb("v_sb", [P, 2, TILES, HEADS, ROW])
        p_sb = sb("p_sb", [P, 4, SLOT])
        k_st = sb("k_st", [P, HEADS, S], bf16)
        q_st = sb("q_st", [P, HEADS, S], bf16)
        scratch = sb("scratch", [P, SLOT])
        k_diag = sb("k_diag", [P, 2, HEADS, SAMPLE], bf16)
        negmax = sb("negmax", [P, HEADS, TILES])
        halfmax = sb("halfmax", [P, P, 2])
        negmax_t = sb("negmax_t", [P, 2, P], bf16)
        state = sb("state", [2, CHUNKS, DH])
        stats = sb("stats", [P, TILES, 6])
        mv = sb("mv", [P, TILES, 2])
        rs = sb("rs", [P, 3, TILES])
        fine = sb("fine", [P, B * 2 * UNITS])
        all_fine = sb("all_fine", [P, 1])
        least = sb("least", [1, 1])
        again = sb("again", [1, 1], i32)

        part_dram = dram("part_dram", (2, 2, 3, P, S), bf16)
        m_dram = dram("m_dram", (2, 2, HEADS, S), bf16)
        ones_dram = dram("ones_dram", (2, GH, S), bf16)
        ffn_dram = dram("ffn_dram", (B, P, TILES, D), f32)

        def c(name):
            return con[:, COLS[name][0]:COLS[name][1]]

        wqk = c("wqk").rearrange("p (i n) -> p i n", i=4)
        bqk = c("bqk")
        wv = c("wv").rearrange("p (a n) -> p a n", a=2)
        bv = c("bv").rearrange("p (a n) -> p a n", a=2)
        wo = c("wo").rearrange("p (a g n) -> p a g n", a=2, g=GROUPS)
        bo = c("bo").rearrange("p (a n) -> p a n", a=2)
        ident = c("ident")
        holt = c("holt")
        holt_state = c("holt_state").rearrange("p (j i) -> p j i", i=2)
        carry = c("carry")[0:2, :]
        carry_state = c("carry_state")[0:2, :]

        def rows(name, k):
            lo, hi = COLS[name]
            return con[:, lo:hi].rearrange("p (k n) -> p k n", k=1).broadcast_to([P, k, hi - lo])

        k_parts = p_sb[:, :, :].rearrange("p i n -> p (i n)").bitcast(bf16)[:, 0:3 * S].rearrange("p (i s) -> p i s", i=3)
        hidden = p_sb[:, :, :].rearrange("p i n -> p (i n)").rearrange("p (m n) -> p m n", m=HB)
        nets = k_st[:, :, :].rearrange("p h s -> p (h s)").bitcast(f32)
        w_ffn_sb, w_ff_sb = nets[:, 0:4 * SLOT], nets[:, 4 * SLOT:8 * SLOT]
        q_flat = q_st[:, :, :].rearrange("p h s -> p (h s)")
        q_parts = q_flat[:, 0:3 * S].rearrange("p (i s) -> p i s", i=3)
        k_all = q_flat[:, 8 * SLOT:8 * SLOT + 2 * S].rearrange("p (i s) -> p i s", i=2)
        tail = q_flat.bitcast(f32)

        def chunk(i):
            return tail[:, i * SLOT:(i + 1) * SLOT].rearrange("p (t n) -> p t n", t=CT)

        second, y4, x4, o4 = chunk(3), chunk(4), chunk(6), chunk(7)
        yt_sb = tail[:, 5 * SLOT:6 * SLOT]
        yt2 = yt_sb.rearrange("p (k n) -> p k n", k=2)

        def net(flat):
            return (flat[:, 0:2 * FF].rearrange("p (k n) -> p k n", k=2),
                    flat[:, 2 * FF:4 * FF].rearrange("p (m n) -> p m n", m=HB))

        slot = [ctx.enter_context(nc.psum_tensor(f"slot{i}", [P, SLOT], f32)) for i in range(4)]
        o_bank = [slot[3][:, i * CHUNK:(i + 1) * CHUNK] for i in range(2)]

        def sem(name):
            return ctx.enter_context(nc.semaphore(name))

        consts_in = sem("consts_in")
        ones_made = sem("ones_made")
        ones_out = sem("ones_out")
        added = sem("added")
        checked = sem("checked")
        flagged = sem("flagged")
        held = sem("held")

        def semaphores(level):
            return Semaphores(lambda name: sem(f"{name}_{level}"))

        def hold(eng, semaphore, value):
            eng.wait_ge(semaphore, value)
            eng.sem_inc(held, 1)

        def batches(eng, prologue, middle, last):
            prologue(0)
            with eng.Fori(0, B - 1) as b:
                middle(b)
            last(B - 1)

        def net_number(b, cc, which):
            if isinstance(b, int) and b == -1:
                return cc
            if isinstance(b, int) and b == B - 1:
                return CHUNKS + 2 * CHUNKS * b + cc
            return CHUNKS + 2 * CHUNKS * b + 2 * cc + (1 - which)

        x_v = x.rearrange("b (t p) d -> b p t d", p=P)
        out_v = out.rearrange("b (t p) d -> b p t d", p=P)

        def one(dram_v, b, cc):
            return dram_v[ds(b, 1), :, ds(cc * CT, CT), :].rearrange("b p t d -> p (b t) d")

        block = ctx.enter_context(nc.Block())
        levels = [(mode, Order(mode), semaphores(n)) for n, mode in enumerate(modes)]

        def run(program, eng):
            program(eng, *levels[0])
            if len(levels) > 1:
                eng.wait_ge(flagged, 1)
                flag = eng.value_load(again[0:1, 0:1], min_val=0, max_val=1)
                with eng.If(flag > 0):
                    program(eng, *levels[1])

        def sync_program(sp, mode, order, s):
            def load_x(b):
                for i in range(CHUNKS):
                    sp.dma_start(xn[:, i * CT:(i + 1) * CT, :], one(x_v, b, i)).then_inc(s.x_in, 16)

            def load_net(dst, src):
                sp.dma_start(dst, src).then_inc(s.nets_in, 16)

            def prologue(b):
                for a in range(2):
                    br = 2 * b + a
                    for which, (parts, out) in enumerate(((k_parts, s.k_out), (q_parts, s.q_out))):
                        hold(sp, s.parts_ready, 4 * br + 2 * which + 2)
                        sp.dma_start(part_dram[a, which].rearrange("i p s -> p i s"), parts).then_inc(out, 16)
                    hold(sp, s.negmax_parts, br + 1)
                    sp.dma_start(m_dram[a].rearrange("i h (t n) -> (h t) i n", t=TILES), negmax_t[:, :, :]).then_inc(s.m_out, 16)

            def results(b, cc):
                n = CHUNKS * b + cc
                hold(sp, s.o_ready, n + 1)
                sp.dma_start(x4, one(ffn_dram, b, cc)).then_inc(s.back_in, 16)
                hold(sp, s.o_ready, n + 2)
                sp.dma_start(one(out_v, b, cc), o4).then_inc(s.stored, 16)

            def attended(b):
                hold(sp, s.pv_done, 2 * UNITS * TILES * (b + 1) + 2)

            def middle(b):
                hold(sp, s.xn_used, b + 1)
                load_x(b + 1)
                attended(b)
                load_net(w_ffn_sb, w_ffn)
                load_net(w_ff_sb, w_ff)
                prologue(b + 1)
                hold(sp, s.second_out, 16 * CHUNKS * (b + 1))
                with sp.Fori(0, CHUNKS) as cc:
                    results(b, cc)

            def last(b):
                attended(b)
                load_net(w_ff_sb, w_ff)
                with sp.Fori(0, CHUNKS) as cc:
                    results(b, cc)

            sp.sem_inc(s.stored, 16)
            load_x(0)
            load_net(w_ffn_sb, w_ffn)
            batches(sp, prologue, middle, last)
            sp.wait_ge(s.second_out, 16 * CHUNKS * B)
            sp.wait_ge(s.stored, 16 * (CHUNKS * B + 1))

        @block.sync
        def _(sp):
            sp.dma_start(con[:, :], packed).then_inc(consts_in, 16)
            sp.wait_ge(ones_made, 1)
            sp.dma_start(ones_dram, q_st[0:2, 0:GH, :]).then_inc(ones_out, 16)
            run(sync_program, sp)

        def pool_program(pool, mode, order, s):
            def second_net(b, cc):
                n = CHUNKS * b + cc
                if not isinstance(n, int) or n > 0:
                    hold(pool, s.second_out, 16 * n)
                pool.dma_start(second, one(x_v, b, cc)).then_inc(s.second_in, 16)
                hold(pool, s.second_ready, n + 2)
                pool.dma_start(one(ffn_dram, b, cc), second).then_inc(s.second_out, 16)

            def fill(b, a, g):
                heads = slice(GH * g, GH * (g + 1))
                for which, (stack, parts) in enumerate(((k_st, K_PART), (q_st, Q_PART))):
                    for r, part in enumerate(parts):
                        src = part_dram[a, which, part, DK * GH * g:DK * GH * (g + 1), :].rearrange("(h d) s -> d h s", d=DK)
                        pool.dma_start(stack[DK * r:DK * (r + 1), heads, :], src).then_inc(s.stack_in[g], 16)
                pool.dma_start(k_st[STACK:ROWS, heads, :], ones_dram).then_inc(s.stack_in[g], 16)
                pool.dma_start(q_st[STACK:ROWS, heads, :], m_dram[a, :, heads, :]).then_inc(s.stack_in[g], 16)

            def first_fill(b):
                hold(pool, s.k_out, 16 * 2 * (b + 1) + 16)
                hold(pool, s.q_out, 16 * 2 * (b + 1) + 16)
                hold(pool, s.m_out, 32 * (b + 1))
                hold(pool, s.second_out, 16 * CHUNKS * (b + 1))
                fill(b, 0, 0)

            def prologue(b):
                for cc in range(CHUNKS):
                    second_net(b, cc)
                first_fill(b)
                fill(b, 0, 1)
                residual(b)

            def residual(b):
                hold(pool, s.work_made, b * order.uses + order.branch[0]["holt"] + 2)
                pool.wait_ge(s.y_ready, CHUNKS * b + 1)
                pool.tensor_tensor(resid[:, :, 0:DH], xn[:, :, 0:DH], bo[:, 0:1, :].broadcast_to([P, TILES, DH]), ALU.add)\
                    .then_inc(s.xn_used, 1)

            def refill(b):
                for g in range(GROUPS):
                    hold(pool, s.pv_done, TILES * (2 * UNITS * b + CHUNKS * (g + 1)) + 2)
                    fill(b, 1, g)

            def middle(b):
                refill(b)
                hold(pool, s.pv_done, TILES * (2 * UNITS * b + UNITS + CHUNKS) + 2)
                with pool.Fori(0, CHUNKS) as cc:
                    second_net(b + 1, cc)
                first_fill(b + 1)
                residual(b + 1)
                hold(pool, s.stored, 16 * (CHUNKS * (b + 1) + 1))
                fill(b + 1, 0, 1)

            def last(b):
                refill(b)

            batches(pool, prologue, middle, last)

        @block.gpsimd
        def _(pool):
            pool.memset(q_st[0:2, 0:GH, :], 1.0).then_inc(ones_made, 1)
            pool.wait_ge(consts_in, 16)
            pool.wait_ge(ones_out, 16)
            run(pool_program, pool)

        def scalar_program(act, mode, order, s):
            def prologue(b):
                for a in range(2):
                    br = 2 * b + a
                    at = order.branch[a]
                    for which, (parts, first) in enumerate(((k_parts, at["k"]), (q_parts, at["q"]))):
                        act.wait_ge(s.q_out if which else s.k_out, 16 * (br + 1))
                        if which == 1 and a == 1:
                            act.wait_ge(s.work_made, b * order.uses + order.branch[0]["turn"])
                        for i in range(2):
                            act.wait_ge(s.work_made, b * order.uses + first + i + 1)
                            act.activation(parts[:, 0, i * SLOT:(i + 1) * SLOT], slot[(first + i) % 4][:, :], ACT.Identity,
                                           bias=bqk[:, 2 * a + which:2 * a + which + 1]).then_inc(s.first_part, 1)

            def activate(b, cc, which):
                n = net_number(b, cc, which)
                act.wait_ge(s.net_done, n + 1)
                bias = c("b1") if which else c("b_ff1")
                for m in range(HB):
                    act.wait_ge(s.hid_made, HB * n + m + 1)
                    act.activation(hidden[:, m, :], slot[m // 2 % 2][:, (m % 2) * CHUNK:(m % 2 + 1) * CHUNK], ACT.Relu,
                                   bias=bias[:, m:m + 1]).then_inc(s.hid_read, 1)

            def attention(b):
                for half in range(2 * GROUPS):
                    with act.Fori(0, CHUNKS // 2) as pair:
                        for i in range(2):
                            u = 2 * UNITS * b + CHUNKS * half + 2 * pair + i
                            for n in range(STEPS):
                                act.wait_ge(s.scores_made, STEPS * u + n + 1)
                                if n % 2 == 0:
                                    act.wait_ge(s.pv_done, TILES * u + n // 2 + 1)
                                act.activation(p_sb[:, n % 4, :], slot[n % 3][:, :], ACT.Exp, scale=0.25).then_inc(s.exp_done, 1)

            def first(b):
                prologue(b)
                hold(act, s.k_out, 16 * 2 * (b + 1) + 16)
                with act.Fori(0, CHUNKS) as cc:
                    activate(-1, cc, 1)

            def middle(b):
                attention(b)
                prologue(b + 1)
                hold(act, s.k_out, 16 * 2 * (b + 2) + 16)
                with act.Fori(0, CHUNKS) as cc:
                    activate(b, cc, 1)
                    activate(b, cc, 0)

            def last(b):
                attention(b)
                with act.Fori(0, CHUNKS) as cc:
                    activate(b, cc, 0)

            act.sem_inc(s.exp_done, 3)
            act.sem_inc(s.hid_read, 4)
            act.sem_inc(s.k_out, 16)
            act.sem_inc(s.q_out, 16)
            batches(act, first, middle, last)

        @block.scalar
        def _(act):
            act.wait_ge(consts_in, 16)
            run(scalar_program, act)

        NEWTON = 4
        RSQRT_STEPS = 3 + 3 * NEWTON

        def vector_program(dve, mode, order, s):
            step = Steps(dve, s.step)

            def rsqrt(n):
                v, r, t = rs[:, 0, 0:n], rs[:, 1, 0:n], rs[:, 2, 0:n]
                step(dve.tensor_scalar(v, mv[:, 0:n, 1], EPS, None, ALU.add))
                step.settle()
                step(dve.tensor_scalar(t.bitcast(i32), v.bitcast(i32), 1, None, ALU.logical_shift_right))
                step.settle()
                step(dve.tensor_scalar(r.bitcast(i32), t.bitcast(i32), -1.0, float(0x5F3759DF), ALU.mult, ALU.add))
                for _ in range(NEWTON):
                    step.settle()
                    step(dve.tensor_tensor(t, r, r, ALU.mult))
                    step.settle()
                    step(dve.scalar_tensor_tensor(t, t, -0.5, v, ALU.mult, ALU.mult))
                    step.settle()
                    step(dve.scalar_tensor_tensor(r, t, 1.5, r, ALU.add, ALU.mult))
                step.settle()

            def normalise(srcs, dsts):
                for i, src in enumerate(srcs):
                    step(dve.bn_stats(stats[:, i, :], src))
                step.settle(hold)
                for i in range(len(srcs)):
                    step(dve.bn_aggr(mv[:, i, :], stats[:, i, :]))
                step.settle()
                rsqrt(len(srcs))
                for i, (src, dst) in enumerate(zip(srcs, dsts)):
                    step(dve.tensor_scalar(dst, src, mv[:, i, 0:1], rs[:, 1, i:i + 1], ALU.subtract, ALU.mult))
                step.settle()

            def norm_steps(n):
                return 3 * n + RSQRT_STEPS

            def layer_norm(b):
                dve.wait_ge(s.x_in, 16 * CHUNKS * (b + 1))
                tiles = [xn[:, t, :] for t in range(TILES)]
                normalise(tiles, tiles)
                dve.memset(state[:, :, :], 0.0).then_inc(s.xn_ready, 1)
                dve.wait_ge(s.xn_ready, b + 1)
                dve.tensor_copy(state[0:1, 0, :], xn[0:1, 0, 0:DH]).then_inc(s.state_saved, 1)

            def prologue(b):
                w0 = b * order.uses

                def made(j):
                    dve.wait_ge(s.work_made, w0 + j + 1)

                for j in range(4):
                    made(j)
                    dst = (xt[:, 0, :] if j < 2 else xt_hi[:, :])[:, (j % 2) * SLOT:(j % 2 + 1) * SLOT]
                    dve.tensor_copy(dst, slot[j][:, :]).then_inc(s.work_read, 1)
                dve.wait_ge(s.o_read, 2 * UNITS * b + 2)
                for a in range(2):
                    br = 2 * b + a
                    at = order.branch[a]

                    def split(which, parts, first):
                        for i in range(2):
                            lo, hi = i * SLOT, (i + 1) * SLOT
                            dve.wait_ge(s.first_part, 4 * br + 2 * which + i + 1)
                            dve.scalar_tensor_tensor(scratch[:, :], slot[(first + i) % 4][:, :], bqk[:, 2 * a + which:2 * a + which + 1],
                                                     parts[:, 0, lo:hi], ALU.add, ALU.subtract).then_inc(s.work_read, 1)
                            dve.wait_ge(s.work_read, w0 + first + i + 1 + 4)
                            step(dve.tensor_copy(parts[:, 1, lo:hi], scratch[:, :]))
                            step.settle()
                            dve.tensor_tensor(parts[:, 2, lo:hi], scratch[:, :], parts[:, 1, lo:hi], ALU.subtract).then_inc(s.parts_ready, 1)
                            dve.wait_ge(s.parts_ready, 4 * br + 2 * which + i + 1)

                    split(0, k_parts, at["k"])
                    if mode == "sample":
                        for i in range(2):
                            dve.tensor_tensor(k_diag[:, i, :, :],
                                              k_parts[:, i:i + 1, 0:S:S // SAMPLE].broadcast_to([P, HEADS, SAMPLE]),
                                              c("own").rearrange("p (h n) -> p h n", n=1).broadcast_to([P, HEADS, SAMPLE]),
                                              ALU.mult).then_inc(s.diag_ready, 1)
                    if at["holt"] is not None:
                        for k in range(1, CHUNKS):
                            dve.wait_ge(s.state_made, (CHUNKS - 1) * b + k)
                            dve.tensor_copy(state[:, k, :], slot[at["state"] % 4][0:2, k * P:(k + 1) * P]).then_inc(s.state_saved, 1)
                        dve.wait_ge(s.state_saved, CHUNKS * (b + 1))
                        dve.sem_inc(s.work_read, 1)
                        for i in range(2):
                            made(at["holt"] + i)
                            dve.tensor_copy(xt[:, 1, i * SLOT:(i + 1) * SLOT], slot[(at["holt"] + i) % 4][:, :]).then_inc(s.work_read, 1)
                    for i in range(4):
                        made(at["v"] + i)
                        dve.tensor_tensor(v_sb[:, a, 4 * i:4 * (i + 1), :, :].rearrange("p t h n -> p t (h n)"),
                                          slot[(at["v"] + i) % 4][:, :].rearrange("p (t n) -> p t n", t=4),
                                          bv[:, a:a + 1, :].broadcast_to([P, 4, HEADS * ROW]), ALU.add).then_inc(s.work_read, 1)
                    split(1, q_parts, at["q"])
                    if mode == "sample":
                        for i in range(4):
                            made(at["max"] + i)
                            ins = dve.tensor_reduce(negmax[:, :, 4 * i:4 * (i + 1)].rearrange("p h t -> p t h"),
                                                    slot[(at["max"] + i) % 4][:, :].rearrange("p (t h k) -> p t h k", h=HEADS, k=SAMPLE),
                                                    AX.X, ALU.max, negate=True)
                            ins.then_inc(s.work_read, 1)
                    else:
                        for h in range(HEADS):
                            dve.wait_ge(s.work_made, w0 + at["max"] + 2 * TILES * h)
                            for i in range(2):
                                dve.tensor_scalar(k_all[:, i, :], k_parts[:, i, :], c("own")[:, h:h + 1], None, ALU.mult)\
                                    .then_inc(s.all_ready, 1)
                            with dve.Fori(0, TILES // 2) as pair:
                                for i in range(4):
                                    j = at["max"] + 2 * TILES * h + i
                                    dve.wait_ge(s.work_made, w0 + j + 4 * pair + 1)
                                    dve.reduce_max(halfmax[:, ds(2 * pair + (TILES * h + i // 2), 1), i % 2], slot[j % 4][:, :], AX.X)\
                                        .then_inc(s.work_read, 1)
                        dve.wait_ge(s.work_read, w0 + at["turn"] + 4)
                        dve.tensor_reduce(negmax[:, :, :].rearrange("p h t -> p (h t)"), halfmax[:, :, :], AX.X, ALU.max, negate=True)\
                            .then_inc(s.negmax_ready, 1)
                    made(at["turn"])
                    src = slot[at["turn"] % 4][:, 0:P]
                    if a == 1 or not isinstance(b, int):
                        dve.wait_ge(s.m_out, 16 * br)
                    step(dve.tensor_copy(negmax_t[:, 0, :], src))
                    step.settle()
                    dve.tensor_tensor(negmax_t[:, 1, :], src, negmax_t[:, 0, :], ALU.subtract).then_inc(s.negmax_parts, 1)
                    dve.wait_ge(s.negmax_parts, br + 1)
                    dve.sem_inc(s.work_read, 1)

            def residual(b):
                for i in range(2):
                    j = order.resid + i
                    dve.wait_ge(s.work_made, b * order.uses + j + 1)
                    dve.tensor_tensor(resid[:, 8 * i:8 * (i + 1), DH:D], slot[j % 4][:, :].rearrange("p (t n) -> p t n", t=8),
                                      bo[:, 1:2, :].broadcast_to([P, 8, DH]), ALU.add).then_inc(s.work_read, 1)

            PER_UNIT = 4

            def attention(b, next_norm):
                den, rden = scratch[:, 0:CHUNK], scratch[:, CHUNK:]
                for a in range(2):
                    for g in range(GROUPS):
                        with step.over(CHUNKS // 2, 2 * PER_UNIT) as pair:
                            for i in range(2):
                                u = 2 * UNITS * b + UNITS * a + CHUNKS * g + 2 * pair + i
                                hold(dve, s.pv_done, TILES * (u + 1) + 2)
                                step(dve.stream_shuffle(den, o_bank[i], [DK] * 32))
                                step.settle()
                                step(dve.reciprocal(rden, den))
                                step.settle()
                                dve.tensor_tensor(att[:, g, ds((2 * pair + i) * CHUNK, CHUNK)], o_bank[i], rden, ALU.mult)\
                                    .then_inc(s.o_read, 1)
                                step(dve.tensor_scalar(den, den, SUM_LIMIT, None, ALU.is_le))
                                step.settle()
                                step(dve.tensor_reduce(fine[:, ds(u, 1)], den, AX.X, ALU.min))
                                step.settle()
                                dve.wait_ge(s.o_read, u + 1 + 2)
                        if a == 0 and g == 0 and next_norm:
                            layer_norm(b + 1)
                    for i in range(2):
                        j = order.out[a] + i
                        if a == 0 and i == 0:
                            dve.wait_ge(s.xn_used, b + 1)
                        dve.wait_ge(s.work_made, b * order.uses + j + 1)
                        half = resid[:, 8 * i:8 * (i + 1), a * DH:(a + 1) * DH]
                        dve.tensor_tensor(half, slot[j % 4][:, :].rearrange("p (t n) -> p t n", t=8), half, ALU.add)\
                            .then_inc(s.work_read, 1)

                dve.wait_ge(s.work_read, (b + 1) * order.uses + 4)

            def second_net(b, n, number):
                dve.wait_ge(s.second_in, 16 * (n + 1))
                dve.wait_ge(s.net_done, number + 2)
                step(dve.tensor_tensor(second, slot[3][:, :].rearrange("p (t n) -> p t n", t=CT), second, ALU.add))
                step.settle()
                dve.tensor_tensor(second, second, rows("b2", CT), ALU.add).then_inc(s.second_ready, 1)

            def first_y(b, cc):
                n = CHUNKS * b + cc
                srcs = [resid[:, ds(cc * CT + t, 1), a * DH:(a + 1) * DH].rearrange("p t n -> p (t n)")
                        for t in range(CT) for a in range(2)]
                normalise(srcs, [y4[:, t, a * DH:(a + 1) * DH] for t in range(CT) for a in range(2)])
                step(dve.tensor_tensor(y4, y4, rows("gamma", CT), ALU.mult))
                step.settle()
                dve.tensor_tensor(y4, y4, rows("beta", CT), ALU.add).then_inc(s.y_ready, 1)
                dve.wait_ge(s.y_ready, n + 2)

            def finish(b, cc, number):
                n = CHUNKS * b + cc
                dve.wait_ge(s.stored, 16 * (n + 1))
                dve.wait_ge(s.net_done, number + 2)
                dve.tensor_tensor(o4, slot[2][:, :].rearrange("p (t n) -> p t n", t=CT), y4, ALU.add).then_inc(s.ff_read, 1)
                dve.wait_ge(s.ff_read, n + 2)
                step(dve.tensor_tensor(o4, o4, rows("b_ff2", CT), ALU.add))
                step.settle()
                tiles = [o4[:, t, :] for t in range(CT)]
                normalise(tiles, tiles)
                step(dve.tensor_tensor(o4, o4, rows("gamma_ff", CT), ALU.mult))
                step.settle()
                dve.wait_ge(s.back_in, 16 * (n + 1))
                dve.tensor_tensor(o4, o4, x4, ALU.add).then_inc(s.o_ready, 1)
                dve.wait_ge(s.o_ready, n + 2)

            def transposed_y(n):
                dve.wait_ge(s.yt_made, n + 1)
                dve.tensor_copy(yt_sb, slot[2][:, :]).then_inc(s.yt_saved, 1)

            per_last = norm_steps(8) + 1 + 1 + norm_steps(4) + 1
            per_chunk = per_last + 1

            def first(b):
                layer_norm(b)
                prologue(b)
                with step.over(CHUNKS, 1) as cc:
                    second_net(b, CHUNKS * b + cc, net_number(-1, cc, 1))
                residual(b)

            def middle(b):
                attention(b, True)
                prologue(b + 1)
                with step.over(CHUNKS, per_chunk) as cc:
                    first_y(b, cc)
                    second_net(b + 1, CHUNKS * (b + 1) + cc, net_number(b, cc, 1))
                    transposed_y(CHUNKS * b + cc)
                    finish(b, cc, net_number(b, cc, 0))
                residual(b + 1)

            def last(b):
                attention(b, False)
                with step.over(CHUNKS, per_last) as cc:
                    first_y(b, cc)
                    transposed_y(CHUNKS * b + cc)
                    finish(b, cc, net_number(b, cc, 0))

            dve.sem_inc(s.work_read, 4)
            dve.sem_inc(s.o_read, 2)
            for semaphore in (s.second_ready, s.y_ready, s.ff_read, s.o_ready):
                dve.sem_inc(semaphore, 1)
            first(0)
            per_middle = (2 * GROUPS * (CHUNKS // 2) * 2 * PER_UNIT + norm_steps(16)) + (2 * 4 + 2) + CHUNKS * per_chunk
            with step.over(B - 1, per_middle) as b:
                middle(b)
            last(B - 1)

        @block.vector
        def _(dve):
            dve.wait_ge(consts_in, 16)
            dve.tensor_tensor(c("b2"), c("b2"), c("beta_ff"), ALU.add).then_inc(added, 1)
            dve.wait_ge(added, 1)
            if len(levels) > 1:
                def check():
                    s = levels[0][2]
                    dve.wait_ge(s.second_out, 16 * CHUNKS * B)
                    dve.wait_ge(s.stored, 16 * (CHUNKS * B + 1))
                    dve.tensor_reduce(all_fine[:, :], fine[:, :], AX.X, ALU.min).then_inc(added, 1)
                    dve.wait_ge(checked, 1)
                    dve.tensor_reduce(least[:, :], slot[0][0:1, 0:P], AX.X, ALU.min).then_inc(added, 1)
                    dve.wait_ge(added, 3)
                    dve.tensor_scalar(again[:, :], least[:, :], 0.5, None, ALU.is_lt).then_inc(flagged, 1)

                vector_program(dve, *levels[0])
                check()
                dve.wait_ge(flagged, 1)
                flag = dve.value_load(again[0:1, 0:1], min_val=0, max_val=1)
                with dve.If(flag > 0):
                    vector_program(dve, *levels[1])
            else:
                vector_program(dve, *levels[0])

        def tensor_program(pe, mode, order, s):
            def prologue(b):
                w0 = b * order.uses

                def free(j):
                    pe.wait_ge(s.work_read, w0 + j + 1)

                def transpose8(j, src):
                    for t in range(8):
                        mm = pe.transpose(slot[j % 4][:, t * P:(t + 1) * P], src(t), ident)
                    mm.then_inc(s.work_made, 1)

                pe.wait_ge(s.work_read, w0 + 4)
                pe.wait_ge(s.xn_ready, b + 1)
                for j in range(4):
                    transpose8(j, lambda t: xn[:, 8 * (j % 2) + t, (j // 2) * DH:(j // 2 + 1) * DH])
                for a in range(2):
                    br = 2 * b + a
                    at = order.branch[a]

                    def project(which, first):
                        for i in range(2):
                            free(first + i)
                            for k in range(2):
                                mm = pe.matmul(slot[(first + i) % 4][:, k * CHUNK:(k + 1) * CHUNK], wqk[:, 2 * a + which, :],
                                               xt[:, a, (2 * i + k) * CHUNK:(2 * i + k + 1) * CHUNK], start=True, stop=True)
                            mm.then_inc(s.work_made, 1)

                    pe.wait_ge(s.work_read, w0 + (2 if a == 0 else order.branch[0]["holt"] + 2) + 4)
                    project(0, at["k"])
                    if at["holt"] is not None:
                        pe.wait_ge(s.work_read, w0 + 4 + 4)
                        for k in range(CHUNKS):
                            j = at["holt"] + k // 2
                            bank = slot[j % 4][:, (k % 2) * CHUNK:(k % 2 + 1) * CHUNK]
                            if k == 0:
                                free(at["state"])
                            if k % 2 == 0:
                                free(j)
                            hold(pe, s.state_saved, CHUNKS * b + k + 1)
                            if k == 1:
                                pe.sem_inc(s.work_made, 1)
                            if k + 1 < CHUNKS:
                                after = slot[at["state"] % 4][0:2, (k + 1) * P:(k + 2) * P]
                                pe.matmul(after, carry_state, state[:, k, :], start=True, stop=False)
                                for t in range(CT):
                                    mm = pe.matmul(after, holt_state[:, t, :], xn[:, CT * k + t, 0:DH], start=False, stop=(t == CT - 1))
                                mm.then_inc(s.state_made, 1)
                            pe.matmul(bank, state[:, k, :], carry, start=True, stop=False)
                            for t in range(CT):
                                mm = pe.matmul(bank[:, t * P:], xn[:, CT * k + t, 0:DH], holt[:, 0:CHUNK - t * P],
                                               start=False, stop=(t == CT - 1))
                            if k % 2:
                                mm.then_inc(s.work_made, 1)
                    for i in range(4):
                        free(at["v"] + i)
                        for t in range(4):
                            tok = 4 * i + t
                            mm = pe.matmul(slot[(at["v"] + i) % 4][:, t * D:(t + 1) * D], xt[:, a, tok * P:(tok + 1) * P], wv[:, a, :],
                                           start=True, stop=True)
                        mm.then_inc(s.work_made, 1)
                    project(1, at["q"])
                    pe.wait_ge(s.parts_ready, 4 * (br + 1))
                    if mode == "sample":
                        pe.wait_ge(s.diag_ready, 2 * (br + 1))
                        for i in range(4):
                            free(at["max"] + i)
                            for t in range(4):
                                tok = slice((4 * i + t) * P, (4 * i + t + 1) * P)
                                for n, (qp, kp) in enumerate(((0, 0), (1, 0), (0, 1))):
                                    mm = pe.matmul(slot[(at["max"] + i) % 4][:, t * D:(t + 1) * D], q_parts[:, qp, tok],
                                                   k_diag[:, kp, :, :].rearrange("p h k -> p (h k)"), start=(n == 0), stop=(n == 2))
                            mm.then_inc(s.work_made, 1)
                    else:
                        for h in range(HEADS):
                            hold(pe, s.all_ready, 2 * HEADS * br + 2 * h + 2)
                            with pe.Fori(0, TILES // 2) as pair:
                                for i in range(4):
                                    j = at["max"] + 2 * TILES * h + i
                                    free(j + 4 * pair)
                                    for k in range(2):
                                        cols = slice((2 * (i % 2) + k) * CHUNK, (2 * (i % 2) + k + 1) * CHUNK)
                                        for n, (qp, kp) in enumerate(((0, 0), (1, 0), (0, 1))):
                                            mm = pe.matmul(slot[j % 4][:, k * CHUNK:(k + 1) * CHUNK],
                                                           q_parts[:, qp, ds((2 * pair + i // 2) * P, P)], k_all[:, kp, cols],
                                                           start=(n == 0), stop=(n == 2))
                                    mm.then_inc(s.work_made, 1)
                        pe.wait_ge(s.negmax_ready, br + 1)
                    pe.wait_ge(s.work_read, w0 + at["turn"] + 4)
                    pe.transpose(slot[at["turn"] % 4][:, 0:P], negmax[:, :, :].rearrange("p h t -> p (h t)"), ident).then_inc(s.work_made, 1)

            def net_hidden(number, w1, src):
                for m in range(HB):
                    pe.wait_ge(s.hid_read, HB * number + m + 1)
                    for k in range(2):
                        mm = pe.matmul(slot[m // 2 % 2][:, (m % 2) * CHUNK:(m % 2 + 1) * CHUNK], w1[:, k, m * P:(m + 1) * P],
                                       src(k), start=(k == 0), stop=(k == 1))
                    mm.then_inc(s.hid_made, 1)

            def net_out(number, sl, w2):
                for t in range(CT):
                    for m in range(HB):
                        if t == 0:
                            pe.wait_ge(s.hid_read, HB * number + m + 1 + 4)
                        mm = pe.matmul(sl[:, t * D:(t + 1) * D], hidden[:, m, t * P:(t + 1) * P], w2[:, m, :],
                                       start=(m == 0), stop=(m == HB - 1))
                mm.then_inc(s.net_done, 1)

            def second_net(b, cc, number):
                w1, w2 = net(w_ffn_sb)
                net_hidden(number, w1, lambda k: (xt[:, 0, :] if k == 0 else xt_hi[:, :])[:, ds(cc * CHUNK, CHUNK)])
                pe.wait_ge(s.second_ready, CHUNKS * b + cc + 1)
                net_out(number, slot[3], w2)

            def first_net(b, cc, number):
                n = CHUNKS * b + cc
                w1, w2 = net(w_ff_sb)
                pe.wait_ge(s.y_ready, n + 2)
                pe.wait_ge(s.ff_read, n + 1)
                for k in range(2):
                    for t in range(CT):
                        mm = pe.transpose(slot[2][:, k * CHUNK + t * P:k * CHUNK + (t + 1) * P], y4[:, t, k * P:(k + 1) * P], ident)
                mm.then_inc(s.yt_made, 1)
                pe.wait_ge(s.yt_saved, n + 1)
                net_hidden(number, w1, lambda k: yt2[:, k, :])
                net_out(number, slot[2], w2)

            def residual(b):
                pe.wait_ge(s.hid_read, HB * CHUNKS * (2 * b + 1) + 4)
                pe.wait_ge(s.y_ready, CHUNKS * b + 1)
                pe.wait_ge(s.ff_read, CHUNKS * b + 1)
                pe.wait_ge(s.second_ready, CHUNKS * (b + 1) + 1)
                for i in range(2):
                    j = order.resid + i
                    for t in range(8):
                        mm = pe.transpose(slot[j % 4][:, t * P:(t + 1) * P], xt[:, 1, (8 * i + t) * P:(8 * i + t + 1) * P], ident)
                    mm.then_inc(s.work_made, 1)
                pe.wait_ge(s.work_read, b * order.uses + order.resid + 2 + 4)

            def attention(b):
                w0 = b * order.uses
                for a in range(2):
                    for g in range(GROUPS):
                        hold(pe, s.stack_in[g], 16 * LOADS * (2 * b + a + 1))
                        with pe.Fori(0, CHUNKS // 2) as pair:
                            for i in range(2):
                                u = 2 * UNITS * b + UNITS * a + CHUNKS * g + 2 * pair + i

                                def scores(kt):
                                    for n in (2 * kt, 2 * kt + 1):
                                        pe.wait_ge(s.exp_done, STEPS * u + {0: -1, 1: 0, 2: 0}.get(n, n - 2) + 3)
                                        for k in range(2):
                                            h = GH * g + 2 * (n % 2) + k
                                            mm = pe.matmul(slot[n % 3][:, k * CHUNK:(k + 1) * CHUNK], k_st[0:ROWS, h, kt * P:(kt + 1) * P],
                                                           q_st[0:ROWS, h, ds((2 * pair + i) * CHUNK, CHUNK)], start=True, stop=True)
                                        mm.then_inc(s.scores_made, 1)

                                scores(0)
                                for kt in range(TILES):
                                    if kt + 1 < TILES:
                                        scores(kt + 1)
                                    if kt == 0:
                                        pe.wait_ge(s.o_read, u + 1)
                                    pe.wait_ge(s.exp_done, STEPS * u + 2 * kt + 2 + 3)
                                    for j in range(GH):
                                        n = 2 * kt + j // 2
                                        mm = pe.matmul(o_bank[i][ROW * j:ROW * (j + 1), :], v_sb[:, a, kt, GH * g + j, :],
                                                       p_sb[:, n % 4, (j % 2) * CHUNK:(j % 2 + 1) * CHUNK],
                                                       start=(kt == 0), stop=(kt == TILES - 1), skip_group_check=True)
                                    mm.then_inc(s.pv_done, 1)
                    pe.wait_ge(s.o_read, 2 * UNITS * b + UNITS * (a + 1) + 2)
                    for i in range(2):
                        j = order.out[a] + i
                        for t in range(8):
                            for g in range(GROUPS):
                                tok = 8 * i + t
                                mm = pe.matmul(slot[j % 4][:, t * P:(t + 1) * P], att[:, g, tok * P:(tok + 1) * P], wo[:, a, g, :],
                                               start=(g == 0), stop=(g == GROUPS - 1))
                        mm.then_inc(s.work_made, 1)
                    pe.wait_ge(s.work_read, w0 + order.out[a] + 2 + 4)

            def first(b):
                prologue(b)
                pe.wait_ge(s.work_read, b * order.uses + order.resid + 4)
                hold(pe, s.nets_in, 16)
                with pe.Fori(0, CHUNKS) as cc:
                    second_net(b, cc, net_number(-1, cc, 1))
                residual(b)

            def middle(b):
                attention(b)
                prologue(b + 1)
                pe.wait_ge(s.work_read, (b + 1) * order.uses + order.resid + 4)
                hold(pe, s.nets_in, 16 * (2 * b + 3))
                with pe.Fori(0, CHUNKS) as cc:
                    second_net(b + 1, cc, net_number(b, cc, 1))
                    first_net(b, cc, net_number(b, cc, 0))
                residual(b + 1)

            def last(b):
                attention(b)
                hold(pe, s.nets_in, 16 * 2 * B)
                with pe.Fori(0, CHUNKS) as cc:
                    first_net(b, cc, net_number(b, cc, 0))

            pe.sem_inc(s.pv_done, 2)
            pe.sem_inc(s.net_done, 1)
            batches(pe, first, middle, last)

        @block.tensor
        def _(pe):
            pe.wait_ge(consts_in, 16)
            tensor_program(pe, *levels[0])
            if len(levels) > 1:
                pe.wait_ge(added, 2)
                pe.transpose(slot[0][0:1, 0:P], all_fine[:, :], ident).then_inc(checked, 1)
                pe.wait_ge(flagged, 1)
                flag = pe.value_load(again[0:1, 0:1], min_val=0, max_val=1)
                with pe.If(flag > 0):
                    tensor_program(pe, *levels[1])


def smoothing_tables():
    a = np.array([[1 - ALPHA, 1 - ALPHA], [-BETA * ALPHA, 1 - BETA * ALPHA]])
    cx = np.array([ALPHA, BETA * ALPHA])
    power = [np.eye(2)]
    for _ in range(CHUNK):
        power.append(a @ power[-1])
    hit = np.array([m @ cx for m in power])
    holt = np.zeros((P, CHUNK))
    for s in range(P):
        holt[s, s:] = hit[:CHUNK - s, 0]
    last = hit[CHUNK - 1::-1][:CHUNK].reshape(CT, P, 2).transpose(1, 0, 2)
    carry = np.array([power[t + 1][0] for t in range(CHUNK)]).T
    return holt, last.reshape(P, 2 * CT), carry, power[CHUNK].T


def kernel(**inputs):
    import concourse.bacc as bacc
    from concourse.bass_utils import run_bass_kernel_spmd

    v = {k: np.asarray(a) for k, a in inputs.items()}
    get = lambda name: v["L0_attn_" + name]
    packed = np.zeros((P, N_COLS), np.float32)

    def put(name, a):
        lo, hi = COLS[name]
        packed[:a.shape[0], lo:hi] = a.reshape(a.shape[0], hi - lo)

    def by_partition(a):
        return np.broadcast_to(a.reshape(1, -1), (P, a.size))

    put("wqk", np.stack([get(w + n).T for n in "12" for w in ("wk", "wq")], 1))
    put("bqk", np.stack([get(w + n) for n in "12" for w in ("bk", "bq")], 1))
    wv = np.zeros((P, 2, HEADS, ROW), np.float32)
    bv = np.zeros((2, HEADS, ROW), np.float32)
    bv[:, :, DK] = 1.0
    wo = np.zeros((GH, ROW, 2, GROUPS, DH), np.float32)
    for i, n in enumerate("12"):
        wv[:, i, :, :DK] = get("wv" + n).T.reshape(DH, HEADS, DK)
        bv[i, :, :DK] = get("bv" + n).reshape(HEADS, DK)
        wo[:, :DK, i] = get("wo" + n).T.reshape(GROUPS, GH, DK, DH).transpose(1, 2, 0, 3)
    put("wv", wv)
    put("bv", by_partition(bv))
    put("wo", wo.reshape(P, -1))
    put("bo", by_partition(np.concatenate([get("bo1"), get("bo2")])))
    put("gamma", by_partition(np.concatenate([get("g1"), get("g2")])))
    put("beta", by_partition(np.concatenate([get("be1"), get("be2")])))
    put("gamma_ff", by_partition(get("g_ff")))
    put("beta_ff", by_partition(get("be_ff")))
    put("b_ff2", by_partition(get("b_ff2")))
    put("b2", by_partition(v["L0_ffn_b2"]))
    put("b_ff1", get("b_ff1").reshape(HB, P).T)
    put("b1", v["L0_ffn_b1"].reshape(HB, P).T)
    put("ident", np.eye(P, dtype=np.float32))
    put("own", np.repeat(np.eye(HEADS, dtype=np.float32), DK, 0))
    for name, table in zip(("holt", "holt_state", "carry", "carry_state"), smoothing_tables()):
        put(name, table)

    def net(w1, w2):
        return np.concatenate([w1.reshape(2, P, FF).transpose(1, 0, 2).reshape(P, -1),
                               w2.reshape(HB, P, D).transpose(1, 0, 2).reshape(P, -1)], 1)

    arrays = {
        "x": np.ascontiguousarray(get("x")),
        "packed": packed,
        "w_ff": net(get("w_ff1").T, get("w_ff2").T),
        "w_ffn": net(v["L0_ffn_W1"], v["L0_ffn_W2"]),
    }
    nc = bacc.Bacc("TRN2", target_bir_lowering=False, num_devices=1)
    args = [nc.dram_tensor(k, a.shape, mybir.dt.from_np(a.dtype), kind="ExternalInput").ap() for k, a in arrays.items()]
    out = nc.dram_tensor("out", (B, S, D), mybir.dt.float32, kind="ExternalOutput").ap()
    build(nc, *args, out)
    return run_bass_kernel_spmd(nc, [arrays], core_ids=[0]).results[0]["out"]
```

```python
import numpy as np
import concourse.bass as bass
from concourse import mybir
from contextlib import ExitStack, contextmanager

B, S, D = 4, 2048, 256
DH = D // 2
HEADS, DK = 8, 16
FF = 1024
EPS = 1e-5
ALPHA, BETA = 0.1, 0.1
P = 128
TILES = S // P
CHUNK = 512
CHUNKS = S // CHUNK
CT = CHUNK // P
GROUPS = 2
GH = HEADS // GROUPS
ROW = P // GH
HB = FF // P
SLOT = 1024
SUM_LIMIT = 1e30

K_PART = [0, 1, 0, 2, 0, 1]
Q_PART = [0, 0, 1, 0, 2, 1]
STACK = DK * len(K_PART)
ROWS = STACK + 2

_WIDTHS = [("wqk", 4 * P), ("bqk", 4), ("wv", 2 * DH), ("bv", 2 * GROUPS), ("wo", 2 * GROUPS * P),
           ("bo", 2 * DH), ("gamma", D), ("beta", D), ("gamma_ff", D), ("beta_ff", D), ("b_ff2", D), ("b2", D),
           ("b_ff1", HB), ("b1", HB), ("ident", P), ("holt", CHUNK), ("holt_state", 2 * CT), ("carry", CHUNK),
           ("carry_state", 2), ("own", HEADS)]
COLS, _at = {}, 0
for _name, _w in _WIDTHS:
    COLS[_name] = (_at, _at + _w)
    _at += _w
N_COLS = _at

ACT_TURN, ACT_HOLT, ACT_VALUES, ACT_BACK = 0, 4, (6, 10), 8
ACT_USES = 12
SAMPLE = 16
MAX_TILES = SLOT // (HEADS * SAMPLE)
MAX_USES = {"sample": TILES * HEADS * SAMPLE // SLOT, "all": HEADS * TILES * 2}
UNITS = GROUPS * CHUNKS
STEPS = 2 * TILES
UNIT_LIST = [(a, g, c) for a in range(2) for g in range(GROUPS) for c in range(CHUNKS)]
LOADS = len(K_PART) * 2 + 2


class Semaphores:

    def __init__(self, new):
        self.x_in = [new(f"x_in_{cc}") for cc in range(CHUNKS)]
        self.xn_ready = new("xn_ready")
        self.xn_used = new("xn_used")
        self.work_made = new("work_made")
        self.work_read = new("work_read")
        self.state_saved = new("state_saved")
        self.state_made = new("state_made")
        self.first_part = new("first_part")
        self.parts_ready = new("parts_ready")
        self.act_saved = new("act_saved")
        self.k_out = new("k_out")
        self.q_out = new("q_out")
        self.diag_ready = new("diag_ready")
        self.all_ready = new("all_ready")
        self.negmax_ready = new("negmax_ready")
        self.negmax_parts = new("negmax_parts")
        self.m_out = new("m_out")
        self.stack_in = [new(f"stack_in_{g}") for g in range(GROUPS)]
        self.scores_made = new("scores_made")
        self.exp_done = new("exp_done")
        self.pv_done = new("pv_done")
        self.o_read = new("o_read")
        self.out_made = new("out_made")
        self.out_read = new("out_read")
        self.nets_in = new("nets_in")
        self.hid_made = new("hid_made")
        self.hid_read = new("hid_read")
        self.net_done = new("net_done")
        self.second_in = new("second_in")
        self.second_ready = new("second_ready")
        self.second_out = new("second_out")
        self.y_ready = new("y_ready")
        self.yt_made = new("yt_made")
        self.yt_saved = new("yt_saved")
        self.ff_read = new("ff_read")
        self.back_in = new("back_in")
        self.o_ready = new("o_ready")
        self.stored = new("stored")
        self.step = new("dve_steps")


class Steps:

    def __init__(self, eng, sem):
        self.eng, self.sem, self.base, self.n = eng, sem, 0, 0

    def __call__(self, instruction):
        self.n += 1
        return instruction.then_inc(self.sem, 1)

    def settle(self, wait=None):
        (wait or self.eng.wait_ge)(*(() if wait is None else (self.eng,)), self.sem, self.base + self.n)

    @contextmanager
    def over(self, times, per):
        base, n = self.base, self.n
        with self.eng.Fori(0, times) as i:
            self.base = base + i * per
            yield i
            assert self.n == n + per, (self.n - n, per)
        self.base, self.n = base, n + times * per


class Order:

    def __init__(self, mode):
        self.n = 0
        self.turn = self.take(4)
        self.branch = []
        for a in range(2):
            k = self.take(2)
            if a == 1:
                self.branch[0]["turn"] = self.take(1)
            state = self.take(1) if a == 0 else None
            holt = self.take(2) if a == 0 else None
            self.branch.append(dict(k=k, state=state, holt=holt, q=self.take(2), v=self.take(2),
                                    back=self.take(2) if a == 0 else None,
                                    max=self.take(MAX_USES[mode]), turn=self.take(1) if a else None))
        self.uses = self.n

    def take(self, k):
        self.n += k
        return self.n - k


def build(nc, x, packed, w_ff, w_ffn, out, modes=("sample", "all")):
    f32, bf16, i32 = mybir.dt.float32, mybir.dt.bfloat16, mybir.dt.int32
    ALU, ACT, AX = mybir.AluOpType, mybir.ActivationFunctionType, mybir.AxisListType
    ds = bass.ds

    ctx = ExitStack()
    with ctx:
        def sb(name, shape, dt=f32):
            return ctx.enter_context(nc.sbuf_tensor(name, shape, dt))

        def dram(name, shape, dt):
            return nc.dram_tensor(name, shape, dt, kind="Internal").ap()

        con = sb("con", [P, N_COLS])
        xn = sb("xn", [P, TILES, D])
        resid = sb("resid", [P, TILES, D])
        xt = sb("xt", [P, 2, S])
        xt_hi = sb("xt_hi", [P, S])
        att = xt
        v_sb = sb("v_sb", [P, 2, TILES, HEADS, ROW])
        p_sb = sb("p_sb", [P, 4, SLOT])
        k_st = sb("k_st", [P, HEADS, S], bf16)
        q_st = sb("q_st", [P, HEADS, S], bf16)
        scratch = sb("scratch", [P, SLOT])
        k_diag = sb("k_diag", [P, HEADS, SAMPLE], bf16)
        negmax = sb("negmax", [P, HEADS, TILES])
        halfmax = sb("halfmax", [P, P, 2])
        negmax_t = sb("negmax_t", [P, 2, P], bf16)
        state = sb("state", [2, CHUNKS, DH])
        stats = sb("stats", [P, TILES, 6])
        mv = sb("mv", [P, TILES, 2])
        rs = sb("rs", [P, 3, TILES])
        fine = sb("fine", [P, B * 2 * UNITS])
        all_fine = sb("all_fine", [P, 1])
        least = sb("least", [1, 1])
        again = sb("again", [1, 1], i32)

        part_dram = dram("part_dram", (2, 2, 3, P, S), bf16)
        m_dram = dram("m_dram", (2, 2, HEADS, S), bf16)
        ones_dram = dram("ones_dram", (2, GH, S), bf16)
        ffn_dram = dram("ffn_dram", (B, P, TILES, D), f32)

        def c(name):
            return con[:, COLS[name][0]:COLS[name][1]]

        wqk = c("wqk").rearrange("p (i n) -> p i n", i=4)
        bqk = c("bqk")
        wv = c("wv").rearrange("p (a n) -> p a n", a=2)
        bv = c("bv")
        wo = c("wo").rearrange("p (a g n) -> p a g n", a=2, g=GROUPS)
        ident = c("ident")
        holt = c("holt")
        holt_state = c("holt_state").rearrange("p (j i) -> p j i", i=2)
        carry = c("carry")[0:2, :]
        carry_state = c("carry_state")[0:2, :]

        def rows(name, k):
            lo, hi = COLS[name]
            return con[:, lo:hi].rearrange("p (k n) -> p k n", k=1).broadcast_to([P, k, hi - lo])

        k_parts = p_sb[:, :, :].rearrange("p i n -> p (i n)").bitcast(bf16)[:, 0:3 * S].rearrange("p (i s) -> p i s", i=3)
        hidden = p_sb[:, :, :].rearrange("p i n -> p (i n)").rearrange("p (m n) -> p m n", m=HB)
        nets = k_st[:, :, :].rearrange("p h s -> p (h s)").bitcast(f32)
        net_halves = nets[:, 0:4 * SLOT], nets[:, 4 * SLOT:8 * SLOT]
        w_ffn_sb, w_ff_sb = net_halves
        q_flat = q_st[:, :, :].rearrange("p h s -> p (h s)")
        q_parts = q_flat[:, 0:3 * S].rearrange("p (i s) -> p i s", i=3)
        k_all = q_flat[:, 8 * SLOT:8 * SLOT + 2 * S].rearrange("p (i s) -> p i s", i=2)
        tail = q_flat.bitcast(f32)

        def chunk(i):
            return tail[:, i * SLOT:(i + 1) * SLOT].rearrange("p (t n) -> p t n", t=CT)

        y4, x4, o4 = chunk(4), chunk(6), chunk(7)
        y_other = chunk(3)
        second = scratch[:, :].rearrange("p (t n) -> p t n", t=CT)
        yt_sb = tail[:, 5 * SLOT:6 * SLOT]
        yt2 = yt_sb.rearrange("p (k n) -> p k n", k=2)

        def net(flat):
            return (flat[:, 0:2 * FF].rearrange("p (k n) -> p k n", k=2),
                    flat[:, 2 * FF:4 * FF].rearrange("p (m n) -> p m n", m=HB))

        slot = [ctx.enter_context(nc.psum_tensor(f"slot{i}", [P, SLOT], f32)) for i in range(4)]
        o_bank = [slot[3][:, i * CHUNK:(i + 1) * CHUNK] for i in range(2)]

        def sem(name):
            return ctx.enter_context(nc.semaphore(name))

        consts_in = sem("consts_in")
        v_rest_made = sem("v_rest_made")
        ones_made = sem("ones_made")
        ones_out = sem("ones_out")
        added = sem("added")
        checked = sem("checked")
        flagged = sem("flagged")
        held = sem("held")

        def semaphores(level):
            return Semaphores(lambda name: sem(f"{name}_{level}"))

        def hold(eng, semaphore, value):
            eng.wait_ge(semaphore, value)
            eng.sem_inc(held, 1)

        def batches(eng, prologue, middle, last):
            prologue(0)
            with eng.Fori(0, B - 1) as b:
                middle(b)
            last(B - 1)

        def net_number(b, cc, which):
            if isinstance(b, int) and b == -1:
                return cc
            if isinstance(b, int) and b == B - 1:
                return CHUNKS + 2 * CHUNKS * b + cc
            return CHUNKS + 2 * CHUNKS * b + 2 * cc + (1 - which)

        x_v = x.rearrange("b (t p) d -> b p t d", p=P)
        out_v = out.rearrange("b (t p) d -> b p t d", p=P)

        def one(dram_v, b, cc):
            return dram_v[ds(b, 1), :, ds(cc * CT, CT), :].rearrange("b p t d -> p (b t) d")

        block = ctx.enter_context(nc.Block())
        levels = [(mode, Order(mode), semaphores(n)) for n, mode in enumerate(modes)]

        def run(program, eng):
            program(eng, *levels[0])
            if len(levels) > 1:
                eng.wait_ge(flagged, 1)
                flag = eng.value_load(again[0:1, 0:1], min_val=0, max_val=1)
                with eng.If(flag > 0):
                    program(eng, *levels[1])

        def sync_program(sp, mode, order, s):
            def load_x(b):
                for i in range(CHUNKS):
                    sp.dma_start(xn[:, i * CT:(i + 1) * CT, :], one(x_v, b, i)).then_inc(s.x_in[i], 16)

            def load_net(dst, src):
                sp.dma_start(dst, src).then_inc(s.nets_in, 16)

            def prologue(b):
                for a in range(2):
                    br = 2 * b + a
                    for which, (parts, out) in enumerate(((k_parts, s.k_out), (q_parts, s.q_out))):
                        hold(sp, s.parts_ready, 4 * br + 2 * which + 2)
                        sp.dma_start(part_dram[a, which].rearrange("i p s -> p i s"), parts).then_inc(out, 16)
                    hold(sp, s.negmax_parts, br + 1)
                    sp.dma_start(m_dram[a].rearrange("i h (t n) -> (h t) i n", t=TILES), negmax_t[:, :, :]).then_inc(s.m_out, 16)

            def results(b, cc):
                n = CHUNKS * b + cc
                hold(sp, s.o_ready, n + 1)
                sp.dma_start(x4, one(ffn_dram, b, cc)).then_inc(s.back_in, 16)
                hold(sp, s.o_ready, n + 2)
                sp.dma_start(one(out_v, b, cc), o4).then_inc(s.stored, 16)

            def attended(b):
                hold(sp, s.pv_done, 2 * UNITS * TILES * (b + 1) + 2)

            def middle(b):
                hold(sp, s.xn_used, b + 1)
                load_x(b + 1)
                attended(b)
                load_net(w_ffn_sb, w_ffn)
                load_net(w_ff_sb, w_ff)
                prologue(b + 1)
                hold(sp, s.second_out, 16 * CHUNKS * (b + 1))
                with sp.Fori(0, CHUNKS) as cc:
                    results(b, cc)

            def last(b):
                hold(sp, s.pv_done, TILES * (2 * UNITS * b + UNITS + CHUNKS) + 2)
                load_net(net_halves[0], w_ff)
                attended(b)
                with sp.Fori(0, CHUNKS) as cc:
                    results(b, cc)

            sp.sem_inc(s.stored, 16)
            load_x(0)
            if s is levels[0][2]:
                sp.dma_start(con[:, :], packed).then_inc(consts_in, 16)
                sp.wait_ge(ones_made, 1)
                sp.dma_start(ones_dram, q_st[0:2, 0:GH, :]).then_inc(ones_out, 16)
            load_net(net_halves[1], w_ffn)
            batches(sp, prologue, middle, last)
            sp.wait_ge(s.second_out, 16 * CHUNKS * B)
            sp.wait_ge(s.stored, 16 * (CHUNKS * B + 1))

        @block.sync
        def _(sp):
            run(sync_program, sp)

        def pool_program(pool, mode, order, s):
            def second_net(b, cc):
                n = CHUNKS * b + cc
                if not isinstance(n, int) or n > 0:
                    hold(pool, s.second_out, 16 * n)
                pool.dma_start(second, one(x_v, b, cc)).then_inc(s.second_in, 16)
                hold(pool, s.second_ready, n + 2)
                pool.dma_start(one(ffn_dram, b, cc), second).then_inc(s.second_out, 16)

            def fill(a, g, stack, parts, which):
                heads = slice(GH * g, GH * (g + 1))
                for r, part in enumerate(parts):
                    src = part_dram[a, which, part, DK * GH * g:DK * GH * (g + 1), :].rearrange("(h d) s -> d h s", d=DK)
                    pool.dma_start(stack[DK * r:DK * (r + 1), heads, :], src).then_inc(s.stack_in[g], 16)
                pool.dma_start(stack[STACK:ROWS, heads, :], m_dram[a, :, heads, :] if which else ones_dram)\
                    .then_inc(s.stack_in[g], 16)

            def fill_k(a, g):
                fill(a, g, k_st, K_PART, 0)

            def fill_q(a, g):
                fill(a, g, q_st, Q_PART, 1)

            def first_q(b):
                hold(pool, s.k_out, 16 * 2 * (b + 1) + 16)
                hold(pool, s.q_out, 16 * 2 * (b + 1) + 16)
                hold(pool, s.m_out, 32 * (b + 1))
                fill_q(0, 0)

            def prologue(b):
                first_q(b)
                fill_k(0, 0)
                for cc in range(CHUNKS):
                    second_net(b, cc)
                fill_k(0, 1)
                fill_q(0, 1)
                residual(b)

            def residual(b):
                hold(pool, s.work_read, b * order.uses + order.branch[0]["back"] + 2 + 4)
                pool.wait_ge(s.y_ready, CHUNKS * b + 1)
                pool.tensor_tensor(resid[:, :, :], xn[:, :, :], rows("bo", TILES), ALU.add).then_inc(s.xn_used, 1)

            def refill(b):
                for g in range(GROUPS):
                    hold(pool, s.pv_done, TILES * (2 * UNITS * b + CHUNKS * (g + 1)) + 2)
                    fill_k(1, g)
                    fill_q(1, g)

            def middle(b):
                refill(b)
                first_q(b + 1)
                with pool.Fori(0, CHUNKS) as cc:
                    second_net(b + 1, cc)
                fill_k(0, 0)
                residual(b + 1)
                hold(pool, s.stored, 16 * (CHUNKS * (b + 1) + 1))
                fill_k(0, 1)
                fill_q(0, 1)

            def last(b):
                refill(b)

            batches(pool, prologue, middle, last)

        @block.gpsimd
        def _(pool):
            pool.memset(q_st[0:2, 0:GH, :], 1.0).then_inc(ones_made, 1)
            for a in range(2):
                pool.memset(v_sb[:, a, :, :, DK:DK + 1], 1.0).then_inc(v_rest_made, 1)
                pool.memset(v_sb[:, a, :, :, DK + 1:], 0.0).then_inc(v_rest_made, 1)
            pool.wait_ge(consts_in, 16)
            pool.wait_ge(ones_out, 16)
            run(pool_program, pool)

        def scalar_program(act, mode, order, s):
            def prologue(b):
                def copy(use, dst, form=lambda flat: flat):
                    act.wait_ge(s.work_made, b * order.uses + use + 1)
                    act.activation(dst, form(slot[use % 4][:, :]), ACT.Identity).then_inc(s.act_saved, 1)

                for j in range(4):
                    copy(j, (xt_hi[:, :] if j < 2 else xt[:, 0, :])[:, (j % 2) * SLOT:(j % 2 + 1) * SLOT])
                for a in range(2):
                    br = 2 * b + a
                    at = order.branch[a]
                    for which, (parts, first) in enumerate(((k_parts, at["k"]), (q_parts, at["q"]))):
                        if which == 1 and a == 0:
                            for i in range(2):
                                copy(at["holt"] + i, xt[:, 1, i * SLOT:(i + 1) * SLOT])
                        act.wait_ge(s.q_out if which else s.k_out, 16 * (br + 1))
                        if which == 1 and a == 1:
                            act.wait_ge(s.work_made, b * order.uses + order.branch[1]["k"])
                        for i in range(2):
                            act.wait_ge(s.work_made, b * order.uses + first + i + 1)
                            act.activation(parts[:, 0, i * SLOT:(i + 1) * SLOT], slot[(first + i) % 4][:, :], ACT.Identity,
                                           bias=bqk[:, 2 * a + which:2 * a + which + 1]).then_inc(s.first_part, 1)
                    for i in range(2):
                        copy(at["v"] + i, v_sb[:, a, 8 * i:8 * (i + 1), :, 0:DK],
                             lambda flat: flat.rearrange("p (t h n) -> p t h n", t=8, n=DK))
                    if a == 0:
                        for i in range(2):
                            copy(at["back"] + i, xn[:, 8 * i:8 * (i + 1), DH:D], lambda flat: flat.rearrange("p (t n) -> p t n", t=8))

            def activate(b, cc, which):
                n = net_number(b, cc, which)
                act.wait_ge(s.net_done, n + 1)
                bias = c("b1") if which else c("b_ff1")
                for m in range(HB):
                    act.wait_ge(s.hid_made, HB * n + m + 1)
                    act.activation(hidden[:, m, :], slot[m // 2 % 2][:, (m % 2) * CHUNK:(m % 2 + 1) * CHUNK], ACT.Relu,
                                   bias=bias[:, m:m + 1]).then_inc(s.hid_read, 1)

            def attention(b):
                for n in range(2 * UNITS * STEPS):
                    act.wait_ge(s.scores_made, 2 * UNITS * STEPS * b + n + 1)
                    if n % 2 == 0:
                        act.wait_ge(s.pv_done, 2 * UNITS * TILES * b + n // 2 + 1)
                    act.activation(p_sb[:, n % 4, :], slot[n % 3][:, :], ACT.Exp, scale=0.25).then_inc(s.exp_done, 1)

            def first(b):
                prologue(b)
                hold(act, s.k_out, 16 * 2 * (b + 1) + 16)
                with act.Fori(0, CHUNKS) as cc:
                    activate(-1, cc, 1)

            def middle(b):
                attention(b)
                prologue(b + 1)
                hold(act, s.k_out, 16 * 2 * (b + 2) + 16)
                with act.Fori(0, CHUNKS) as cc:
                    activate(b, cc, 1)
                    activate(b, cc, 0)

            def last(b):
                attention(b)
                with act.Fori(0, CHUNKS) as cc:
                    activate(b, cc, 0)

            act.sem_inc(s.exp_done, 3)
            act.sem_inc(s.hid_read, 4)
            act.sem_inc(s.k_out, 16)
            act.sem_inc(s.q_out, 16)
            batches(act, first, middle, last)

        @block.scalar
        def _(act):
            act.wait_ge(consts_in, 16)
            act.wait_ge(ones_out, 16)
            run(scalar_program, act)

        NEWTON = 3
        RSQRT_STEPS = 3 + 3 * NEWTON

        def vector_program(dve, mode, order, s):
            step = Steps(dve, s.step)

            def rsqrt(n):
                v, r, t = rs[:, 0, 0:n], rs[:, 1, 0:n], rs[:, 2, 0:n]
                step(dve.tensor_scalar(v, mv[:, 0:n, 1], EPS, None, ALU.add))
                step.settle()
                step(dve.tensor_scalar(t.bitcast(i32), v.bitcast(i32), 1, None, ALU.logical_shift_right))
                step.settle()
                step(dve.tensor_scalar(r.bitcast(i32), t.bitcast(i32), -1.0, float(0x5F3759DF), ALU.mult, ALU.add))
                for _ in range(NEWTON):
                    step.settle()
                    step(dve.tensor_tensor(t, r, r, ALU.mult))
                    step.settle()
                    step(dve.scalar_tensor_tensor(t, t, -0.5, v, ALU.mult, ALU.mult))
                    step.settle()
                    step(dve.scalar_tensor_tensor(r, t, 1.5, r, ALU.add, ALU.mult))
                step.settle()

            def normalise(srcs, dsts, arrived=None):
                for i, src in enumerate(srcs):
                    if arrived:
                        arrived(i)
                    step(dve.bn_stats(stats[:, i, :], src))
                step.settle(hold)
                for i in range(len(srcs)):
                    step(dve.bn_aggr(mv[:, i, :], stats[:, i, :]))
                step.settle()
                rsqrt(len(srcs))
                for i, (src, dst) in enumerate(zip(srcs, dsts)):
                    step(dve.tensor_scalar(dst, src, mv[:, i, 0:1], rs[:, 1, i:i + 1], ALU.subtract, ALU.mult))
                step.settle()

            def norm_steps(n):
                return 3 * n + RSQRT_STEPS

            def layer_norm(b):
                tiles = [xn[:, t, :] for t in range(TILES)]
                normalise(tiles, tiles, arrived=lambda t: t % CT or dve.wait_ge(s.x_in[t // CT], 16 * (b + 1)))
                dve.memset(state[:, :, :], 0.0).then_inc(s.xn_ready, 1)
                dve.wait_ge(s.xn_ready, b + 1)
                dve.tensor_copy(state[0:1, 0, :], xn[0:1, 0, 0:DH]).then_inc(s.state_saved, 1)

            def prologue(b, before=None):
                w0 = b * order.uses

                def made(j):
                    dve.wait_ge(s.work_made, w0 + j + 1)

                def pass_on(use):
                    dve.wait_ge(s.act_saved, ACT_USES * b + use + 1)
                    dve.sem_inc(s.work_read, 1)

                def turn(a):
                    place = order.branch[a]["turn"]
                    made(place)
                    src = slot[place % 4][:, 0:P]
                    if a == 1 or not isinstance(b, int):
                        dve.wait_ge(s.m_out, 16 * (2 * b + a))
                    step(dve.tensor_copy(negmax_t[:, 0, :], src))
                    step.settle()
                    dve.tensor_tensor(negmax_t[:, 1, :], src, negmax_t[:, 0, :], ALU.subtract).then_inc(s.negmax_parts, 1)
                    dve.wait_ge(s.negmax_parts, 2 * b + a + 1)
                    dve.sem_inc(s.work_read, 1)

                for j in range(4):
                    if j == 2 and before is not None:
                        out_projection(before, 1)
                    pass_on(ACT_TURN + j)
                dve.wait_ge(s.o_read, 2 * UNITS * b + 2)
                for a in range(2):
                    br = 2 * b + a
                    at = order.branch[a]

                    def save_state(k):
                        dve.wait_ge(s.state_made, (CHUNKS - 1) * b + k)
                        dve.tensor_copy(state[:, k, :], slot[at["state"] % 4][0:2, k * P:(k + 1) * P]).then_inc(s.state_saved, 1)

                    def split(which, parts, first, halves=range(2)):
                        for i in halves:
                            lo, hi = i * SLOT, (i + 1) * SLOT
                            dve.wait_ge(s.first_part, 4 * br + 2 * which + i + 1)
                            dve.scalar_tensor_tensor(scratch[:, :], slot[(first + i) % 4][:, :], bqk[:, 2 * a + which:2 * a + which + 1],
                                                     parts[:, 0, lo:hi], ALU.add, ALU.subtract).then_inc(s.work_read, 1)
                            dve.wait_ge(s.work_read, w0 + first + i + 1 + 4)
                            step(dve.tensor_copy(parts[:, 1, lo:hi], scratch[:, :]))
                            step.settle()
                            dve.tensor_tensor(parts[:, 2, lo:hi], scratch[:, :], parts[:, 1, lo:hi], ALU.subtract).then_inc(s.parts_ready, 1)
                            dve.wait_ge(s.parts_ready, 4 * br + 2 * which + i + 1)

                    split(0, k_parts, at["k"], range(1))
                    if at["holt"] is not None:
                        save_state(1)
                    split(0, k_parts, at["k"], range(1, 2))
                    if a == 1:
                        turn(0)
                    if mode == "sample":
                        dve.tensor_tensor(k_diag[:, :, :], k_parts[:, 0:1, 0:S:S // SAMPLE].broadcast_to([P, HEADS, SAMPLE]),
                                          c("own").rearrange("p (h n) -> p h n", n=1).broadcast_to([P, HEADS, SAMPLE]),
                                          ALU.mult).then_inc(s.diag_ready, 1)
                    if at["holt"] is not None:
                        for k in range(2, CHUNKS):
                            save_state(k)
                        dve.wait_ge(s.state_saved, CHUNKS * (b + 1))
                        dve.sem_inc(s.work_read, 1)
                        for i in range(2):
                            pass_on(ACT_HOLT + i)
                    split(1, q_parts, at["q"])
                    for i in range(2):
                        pass_on(ACT_VALUES[a] + i)
                    if a == 0:
                        for i in range(2):
                            pass_on(ACT_BACK + i)
                    if mode == "sample":
                        for i in range(MAX_USES[mode]):
                            made(at["max"] + i)
                            ins = dve.tensor_reduce(negmax[:, :, MAX_TILES * i:MAX_TILES * (i + 1)].rearrange("p h t -> p t h"),
                                                    slot[(at["max"] + i) % 4][:, :].rearrange("p (t h k) -> p t h k", h=HEADS, k=SAMPLE),
                                                    AX.X, ALU.max, negate=True)
                            ins.then_inc(s.work_read, 1)
                    else:
                        for h in range(HEADS):
                            dve.wait_ge(s.work_made, w0 + at["max"] + 2 * TILES * h)
                            for i in range(2):
                                dve.tensor_scalar(k_all[:, i, :], k_parts[:, i, :], c("own")[:, h:h + 1], None, ALU.mult)\
                                    .then_inc(s.all_ready, 1)
                            with dve.Fori(0, TILES // 2) as pair:
                                for i in range(4):
                                    j = at["max"] + 2 * TILES * h + i
                                    dve.wait_ge(s.work_made, w0 + j + 4 * pair + 1)
                                    dve.reduce_max(halfmax[:, ds(2 * pair + (TILES * h + i // 2), 1), i % 2], slot[j % 4][:, :], AX.X)\
                                        .then_inc(s.work_read, 1)
                        dve.wait_ge(s.work_read, w0 + at["max"] + MAX_USES[mode] + 4)
                        dve.tensor_reduce(negmax[:, :, :].rearrange("p h t -> p (h t)"), halfmax[:, :, :], AX.X, ALU.max, negate=True)\
                            .then_inc(s.negmax_ready, 1)
                    if a == 1:
                        turn(1)

            def out_projection(b, a, chunks=range(CHUNKS)):
                for i in chunks:
                    dve.wait_ge(s.out_made, CHUNKS * (2 * b + a) + i + 1)
                    part = resid[:, CT * i:CT * (i + 1), a * DH:(a + 1) * DH]
                    bank = o_bank[1 if a == 0 else i % 2]
                    dve.tensor_tensor(part, bank.rearrange("p (t n) -> p t n", t=CT), part, ALU.add).then_inc(s.out_read, 1)


            def attention(b, next_norm):
                dve.wait_ge(s.second_out, 16 * CHUNKS * (b + 1))
                den, rden = scratch[:, 0:CHUNK], scratch[:, CHUNK:]
                for n, (a, g, c_) in enumerate(UNIT_LIST):
                    u = 2 * UNITS * b + n
                    if n == UNITS:
                        dve.wait_ge(s.xn_used, b + 1)
                        out_projection(b, 0)
                    hold(dve, s.pv_done, TILES * (u + 1) + 2)
                    step(dve.stream_shuffle(den, o_bank[n % 2], [DK] * 32))
                    step.settle()
                    step(dve.reciprocal(rden, den))
                    step.settle()
                    att_unit = att[:, g, c_ * CHUNK:(c_ + 1) * CHUNK]
                    step(dve.tensor_tensor(att_unit, o_bank[n % 2], rden, ALU.mult))
                    step.settle()
                    dve.tensor_scalar(att_unit, att_unit, bv[:, GROUPS * a + g:GROUPS * a + g + 1], None, ALU.add)\
                        .then_inc(s.o_read, 1)
                    step(dve.tensor_scalar(den, den, SUM_LIMIT, None, ALU.is_le))
                    step.settle()
                    step(dve.scalar_tensor_tensor(den, rden, SUM_LIMIT, den, ALU.is_le, ALU.mult))
                    step.settle()
                    step(dve.tensor_reduce(fine[:, ds(u, 1)], den, AX.X, ALU.min))
                    step.settle()
                    dve.wait_ge(s.o_read, u + 1 + 2)
                    if n == CHUNKS - 1 and next_norm:
                        layer_norm(b + 1)

            def residuals_whole(b, chunks=CHUNKS):
                hold(dve, s.out_read, CHUNKS * (2 * b + 1) + chunks + 1)

            def second_net(b, n, number):
                dve.wait_ge(s.second_in, 16 * (n + 1))
                dve.wait_ge(s.net_done, number + 2)
                step(dve.tensor_tensor(second, slot[3][:, :].rearrange("p (t n) -> p t n", t=CT), second, ALU.add))
                step.settle()
                dve.tensor_tensor(second, second, rows("b2", CT), ALU.add).then_inc(s.second_ready, 1)

            def first_y(b, cc, y4=y4):
                n = CHUNKS * b + cc
                srcs = [resid[:, ds(cc * CT + t, 1), a * DH:(a + 1) * DH].rearrange("p t n -> p (t n)")
                        for t in range(CT) for a in range(2)]
                normalise(srcs, [y4[:, t, a * DH:(a + 1) * DH] for t in range(CT) for a in range(2)])
                step(dve.tensor_tensor(y4, y4, rows("gamma", CT), ALU.mult))
                step.settle()
                dve.tensor_tensor(y4, y4, rows("beta", CT), ALU.add).then_inc(s.y_ready, 1)
                dve.wait_ge(s.y_ready, n + 2)

            def finish(b, cc, number, y4=y4, bank=slot[2]):
                n = CHUNKS * b + cc
                dve.wait_ge(s.stored, 16 * (n + 1))
                dve.wait_ge(s.net_done, number + 2)
                dve.tensor_tensor(o4, bank[:, :].rearrange("p (t n) -> p t n", t=CT), y4, ALU.add).then_inc(s.ff_read, 1)
                dve.wait_ge(s.ff_read, n + 2)
                step(dve.tensor_tensor(o4, o4, rows("b_ff2", CT), ALU.add))
                step.settle()
                tiles = [o4[:, t, :] for t in range(CT)]
                normalise(tiles, tiles)
                step(dve.tensor_tensor(o4, o4, rows("gamma_ff", CT), ALU.mult))
                step.settle()
                dve.wait_ge(s.back_in, 16 * (n + 1))
                dve.tensor_tensor(o4, o4, x4, ALU.add).then_inc(s.o_ready, 1)
                dve.wait_ge(s.o_ready, n + 2)

            def transposed_y(n, bank=slot[2]):
                dve.wait_ge(s.yt_made, n + 1)
                dve.tensor_copy(yt_sb, bank[:, :]).then_inc(s.yt_saved, 1)

            per_chunk = norm_steps(8) + 1 + 1 + norm_steps(4) + 1 + 1

            def first(b):
                layer_norm(b)
                if s is levels[0][2]:
                    dve.wait_ge(consts_in, 16)
                    dve.tensor_tensor(c("b2"), c("b2"), c("beta_ff"), ALU.add).then_inc(added, 1)
                    dve.wait_ge(added, 1)
                prologue(b)
                with step.over(CHUNKS, 1) as cc:
                    second_net(b, CHUNKS * b + cc, net_number(-1, cc, 1))

            def middle(b):
                attention(b, True)
                prologue(b + 1, b)
                residuals_whole(b)
                with step.over(CHUNKS, per_chunk) as cc:
                    first_y(b, cc)
                    transposed_y(CHUNKS * b + cc)
                    second_net(b + 1, CHUNKS * (b + 1) + cc, net_number(b, cc, 1))
                    finish(b, cc, net_number(b, cc, 0))

            def last(b):
                attention(b, False)
                out_projection(b, 1, range(1))
                residuals_whole(b, 1)
                first_y(b, 0)
                out_projection(b, 1, range(1, CHUNKS))
                residuals_whole(b)
                transposed_y(CHUNKS * b)
                for cc in range(CHUNKS):
                    if cc + 1 < CHUNKS:
                        first_y(b, cc + 1, (y4, y_other)[(cc + 1) % 2])
                        transposed_y(CHUNKS * b + cc + 1, slot[2 + (cc + 1) % 2])
                    finish(b, cc, net_number(b, cc, 0), (y4, y_other)[cc % 2], slot[2 + cc % 2])

            dve.sem_inc(s.work_read, 4)
            dve.sem_inc(s.o_read, 2)
            for semaphore in (s.second_ready, s.y_ready, s.ff_read, s.o_ready, s.out_read):
                dve.sem_inc(semaphore, 1)
            first(0)
            per_middle = (2 * UNITS * 6 + norm_steps(16)) + (2 * 4 + 2) + CHUNKS * per_chunk
            with step.over(B - 1, per_middle) as b:
                middle(b)
            last(B - 1)

        @block.vector
        def _(dve):
            if len(levels) > 1:
                def check():
                    s = levels[0][2]
                    dve.wait_ge(s.second_out, 16 * CHUNKS * B)
                    dve.wait_ge(s.stored, 16 * (CHUNKS * B + 1))
                    dve.tensor_reduce(all_fine[:, :], fine[:, :], AX.X, ALU.min).then_inc(added, 1)
                    dve.wait_ge(checked, 1)
                    dve.tensor_reduce(least[:, :], slot[0][0:1, 0:P], AX.X, ALU.min).then_inc(added, 1)
                    dve.wait_ge(added, 3)
                    dve.tensor_scalar(again[:, :], least[:, :], 0.5, None, ALU.is_lt).then_inc(flagged, 1)

                vector_program(dve, *levels[0])
                check()
                dve.wait_ge(flagged, 1)
                flag = dve.value_load(again[0:1, 0:1], min_val=0, max_val=1)
                with dve.If(flag > 0):
                    vector_program(dve, *levels[1])
            else:
                vector_program(dve, *levels[0])

        def tensor_program(pe, mode, order, s):
            def prologue(b, before=None):
                w0 = b * order.uses

                def free(j):
                    pe.wait_ge(s.work_read, w0 + j + 1)

                def transpose8(j, src):
                    for t in range(8):
                        mm = pe.transpose(slot[j % 4][:, t * P:(t + 1) * P], src(t), ident)
                    mm.then_inc(s.work_made, 1)

                def turn(a):
                    at = order.branch[a]
                    pe.wait_ge(s.work_read, w0 + at["max"] + MAX_USES[mode] + 4)
                    free(at["turn"])
                    pe.transpose(slot[at["turn"] % 4][:, 0:P], negmax[:, :, :].rearrange("p h t -> p (h t)"), ident).then_inc(s.work_made, 1)

                pe.wait_ge(s.work_read, w0 + 4)
                pe.wait_ge(s.xn_ready, b + 1)
                for j in range(4):
                    if j == 2 and before is not None:
                        for i in range(CHUNKS):
                            out_projection(before, 1, i)
                    if j == 3:
                        pe.wait_ge(s.out_read, 2 * CHUNKS * b + 1)
                    transpose8(j, lambda t: xn[:, 8 * (j % 2) + t, (1 - j // 2) * DH:(2 - j // 2) * DH])
                for a in range(2):
                    br = 2 * b + a
                    at = order.branch[a]

                    def project(which, first):
                        for i in range(2):
                            free(first + i)
                            for k in range(2):
                                mm = pe.matmul(slot[(first + i) % 4][:, k * CHUNK:(k + 1) * CHUNK], wqk[:, 2 * a + which, :],
                                               xt[:, a, (2 * i + k) * CHUNK:(2 * i + k + 1) * CHUNK], start=True, stop=True)
                            mm.then_inc(s.work_made, 1)

                    pe.wait_ge(s.work_read, w0 + (4 if a == 0 else order.branch[0]["holt"] + 2) + 4)
                    project(0, at["k"])
                    if a == 1:
                        turn(0)
                    if at["holt"] is not None:
                        for k in range(CHUNKS):
                            j = at["holt"] + k // 2
                            bank = slot[j % 4][:, (k % 2) * CHUNK:(k % 2 + 1) * CHUNK]
                            if k == 0:
                                free(at["state"])
                            if k % 2 == 0:
                                free(j)
                            hold(pe, s.state_saved, CHUNKS * b + k + 1)
                            if k == 1:
                                pe.sem_inc(s.work_made, 1)
                            if k + 1 < CHUNKS:
                                after = slot[at["state"] % 4][0:2, (k + 1) * P:(k + 2) * P]
                                pe.matmul(after, carry_state, state[:, k, :], start=True, stop=False)
                                for t in range(CT):
                                    mm = pe.matmul(after, holt_state[:, t, :], xn[:, CT * k + t, 0:DH], start=False, stop=(t == CT - 1))
                                mm.then_inc(s.state_made, 1)
                            pe.matmul(bank, state[:, k, :], carry, start=True, stop=False)
                            for t in range(CT):
                                mm = pe.matmul(bank[:, t * P:], xn[:, CT * k + t, 0:DH], holt[:, 0:CHUNK - t * P],
                                               start=False, stop=(t == CT - 1))
                            if k % 2:
                                mm.then_inc(s.work_made, 1)
                    project(1, at["q"])
                    for i in range(2):
                        free(at["v"] + i)
                        for t in range(8):
                            tok = 8 * i + t
                            mm = pe.matmul(slot[(at["v"] + i) % 4][:, t * P:(t + 1) * P], xt[:, a, tok * P:(tok + 1) * P], wv[:, a, :],
                                           start=True, stop=True)
                        mm.then_inc(s.work_made, 1)
                    if a == 0:
                        for i in range(2):
                            free(at["back"] + i)
                            transpose8(at["back"] + i, lambda t: xt[:, 1, (8 * i + t) * P:(8 * i + t + 1) * P])
                    if mode == "sample":
                        pe.wait_ge(s.first_part, 4 * (br + 1))
                        pe.wait_ge(s.diag_ready, br + 1)
                        for i in range(MAX_USES[mode]):
                            free(at["max"] + i)
                            for t in range(MAX_TILES):
                                tok = slice((MAX_TILES * i + t) * P, (MAX_TILES * i + t + 1) * P)
                                cols = slice(t * HEADS * SAMPLE, (t + 1) * HEADS * SAMPLE)
                                mm = pe.matmul(slot[(at["max"] + i) % 4][:, cols], q_parts[:, 0, tok],
                                               k_diag[:, :, :].rearrange("p h k -> p (h k)"), start=True, stop=True)
                            mm.then_inc(s.work_made, 1)
                    else:
                        pe.wait_ge(s.parts_ready, 4 * (br + 1))
                        for h in range(HEADS):
                            hold(pe, s.all_ready, 2 * HEADS * br + 2 * h + 2)
                            with pe.Fori(0, TILES // 2) as pair:
                                for i in range(4):
                                    j = at["max"] + 2 * TILES * h + i
                                    free(j + 4 * pair)
                                    for k in range(2):
                                        cols = slice((2 * (i % 2) + k) * CHUNK, (2 * (i % 2) + k + 1) * CHUNK)
                                        for n, (qp, kp) in enumerate(((0, 0), (1, 0), (0, 1))):
                                            mm = pe.matmul(slot[j % 4][:, k * CHUNK:(k + 1) * CHUNK],
                                                           q_parts[:, qp, ds((2 * pair + i // 2) * P, P)], k_all[:, kp, cols],
                                                           start=(n == 0), stop=(n == 2))
                                    mm.then_inc(s.work_made, 1)
                        pe.wait_ge(s.negmax_ready, br + 1)
                    if a == 1:
                        turn(1)

            def net_hidden(number, w1, src):
                for m in range(HB):
                    pe.wait_ge(s.hid_read, HB * number + m + 1)
                    for k in range(2):
                        mm = pe.matmul(slot[m // 2 % 2][:, (m % 2) * CHUNK:(m % 2 + 1) * CHUNK], w1[:, k, m * P:(m + 1) * P],
                                       src(k), start=(k == 0), stop=(k == 1))
                    mm.then_inc(s.hid_made, 1)

            def net_out(number, sl, w2, between=None):
                for t in range(CT):
                    if t == CT - 1 and between:
                        between()
                    for m in range(HB):
                        if t == 0:
                            pe.wait_ge(s.hid_read, HB * number + m + 1 + 4)
                        mm = pe.matmul(sl[:, t * D:(t + 1) * D], hidden[:, m, t * P:(t + 1) * P], w2[:, m, :],
                                       start=(m == 0), stop=(m == HB - 1))
                mm.then_inc(s.net_done, 1)

            def second_net(b, cc, number, w, between=None):
                w1, w2 = net(w)
                net_hidden(number, w1, lambda k: (xt[:, 0, :] if k == 0 else xt_hi[:, :])[:, ds(cc * CHUNK, CHUNK)])
                pe.wait_ge(s.second_ready, CHUNKS * b + cc + 1)
                pe.wait_ge(s.work_read, (b + 1) * order.uses + 4)
                net_out(number, slot[3], w2, between)

            def transpose_y(n, y, bank, read):
                pe.wait_ge(s.y_ready, n + 2)
                pe.wait_ge(s.ff_read, read)
                for k in range(2):
                    for t in range(CT):
                        mm = pe.transpose(bank[:, k * CHUNK + t * P:k * CHUNK + (t + 1) * P], y[:, t, k * P:(k + 1) * P], ident)
                mm.then_inc(s.yt_made, 1)

            def first_net(n, number, w, bank, between=None):
                w1, w2 = net(w)
                pe.wait_ge(s.yt_saved, n + 1)
                net_hidden(number, w1, lambda k: yt2[:, k, :])
                net_out(number, bank, w2, between)

            def slots_free(b):
                pe.wait_ge(s.hid_read, HB * CHUNKS * (2 * b + 1) + 4)
                pe.wait_ge(s.ff_read, CHUNKS * b + 1)
                pe.wait_ge(s.second_ready, CHUNKS * (b + 1) + 1)

            def out_projection(b, a, i):
                if i == 0:
                    pe.wait_ge(s.o_read, UNITS * (2 * b + a + 1) + 2)
                pe.wait_ge(s.out_read, CHUNKS * (2 * b + a) + i + (1 if a == 0 else 0))
                bank = o_bank[1 if a == 0 else i % 2]
                for t in range(CT):
                    tok = CT * i + t
                    for g in range(GROUPS):
                        mm = pe.matmul(bank[:, t * P:(t + 1) * P], att[:, g, tok * P:(tok + 1) * P], wo[:, a, g, :],
                                       start=(g == 0), stop=(g == GROUPS - 1))
                mm.then_inc(s.out_made, 1)

            def attention(b):
                def scores(unit, kt):
                    a, g, c_ = UNIT_LIST[unit]
                    if kt == 0 and c_ == 0:
                        hold(pe, s.stack_in[g], 16 * LOADS * (2 * b + a + 1))
                    for n in (2 * kt, 2 * kt + 1):
                        at = STEPS * unit + n
                        pe.wait_ge(s.exp_done, 2 * UNITS * STEPS * b + at - 2 + 3)
                        for k in range(2):
                            h = GH * g + 2 * (n % 2) + k
                            mm = pe.matmul(slot[at % 3][:, k * CHUNK:(k + 1) * CHUNK], k_st[0:ROWS, h, kt * P:(kt + 1) * P],
                                           q_st[0:ROWS, h, c_ * CHUNK:(c_ + 1) * CHUNK], start=True, stop=True)
                        mm.then_inc(s.scores_made, 1)

                scores(0, 0)
                for unit, (a, g, c_) in enumerate(UNIT_LIST):
                    u = 2 * UNITS * b + unit
                    for kt in range(TILES):
                        if kt + 1 < TILES:
                            scores(unit, kt + 1)
                        elif unit + 1 < len(UNIT_LIST):
                            scores(unit + 1, 0)
                        if kt == 0:
                            pe.wait_ge(s.o_read, u + 1)
                            if unit == UNITS + 1:
                                pe.wait_ge(s.out_read, CHUNKS * (2 * b + 1) + 1)
                        pe.wait_ge(s.exp_done, STEPS * u + 2 * kt + 2 + 3)
                        for j in range(GH):
                            n = 2 * kt + j // 2
                            mm = pe.matmul(o_bank[unit % 2][ROW * j:ROW * (j + 1), :], v_sb[:, a, kt, GH * g + j, :],
                                           p_sb[:, n % 4, (j % 2) * CHUNK:(j % 2 + 1) * CHUNK],
                                           start=(kt == 0), stop=(kt == TILES - 1), skip_group_check=True)
                        mm.then_inc(s.pv_done, 1)
                        if unit == UNITS and kt % 3 == 0 and 0 < kt <= 3 * CHUNKS:
                            out_projection(b, 0, kt // 3 - 1)

            def first(b):
                prologue(b)
                hold(pe, s.nets_in, 16)
                with pe.Fori(0, CHUNKS) as cc:
                    second_net(b, cc, net_number(-1, cc, 1), net_halves[1])
                slots_free(b)
                pe.wait_ge(v_rest_made, 4)

            def middle(b):
                attention(b)
                prologue(b + 1, b)
                hold(pe, s.nets_in, 16 * (2 * b + 3))
                with pe.Fori(0, CHUNKS) as cc:
                    n = CHUNKS * b + cc
                    second_net(b + 1, cc, net_number(b, cc, 1), w_ffn_sb, lambda: transpose_y(n, y4, slot[2], n + 1))
                    first_net(n, net_number(b, cc, 0), w_ff_sb, slot[2])
                slots_free(b + 1)

            def last(b):
                attention(b)
                for i in range(CHUNKS):
                    out_projection(b, 1, i)
                hold(pe, s.nets_in, 16 * 2 * B)
                n = CHUNKS * b
                transpose_y(n, y4, slot[2], n + 1)
                pe.wait_ge(s.out_read, 2 * CHUNKS * B + 1)
                for cc in range(CHUNKS):
                    after = cc + 1
                    ahead = lambda: transpose_y(n + after, (y4, y_other)[after % 2], slot[2 + after % 2], n + after)
                    first_net(n + cc, net_number(b, cc, 0), net_halves[0], slot[2 + cc % 2], ahead if after < CHUNKS else None)

            pe.sem_inc(s.pv_done, 2)
            pe.sem_inc(s.net_done, 1)
            batches(pe, first, middle, last)

        @block.tensor
        def _(pe):
            pe.wait_ge(consts_in, 16)
            tensor_program(pe, *levels[0])
            if len(levels) > 1:
                pe.wait_ge(added, 2)
                pe.transpose(slot[0][0:1, 0:P], all_fine[:, :], ident).then_inc(checked, 1)
                pe.wait_ge(flagged, 1)
                flag = pe.value_load(again[0:1, 0:1], min_val=0, max_val=1)
                with pe.If(flag > 0):
                    tensor_program(pe, *levels[1])


def smoothing_tables():
    a = np.array([[1 - ALPHA, 1 - ALPHA], [-BETA * ALPHA, 1 - BETA * ALPHA]])
    cx = np.array([ALPHA, BETA * ALPHA])
    power = [np.eye(2)]
    for _ in range(CHUNK):
        power.append(a @ power[-1])
    hit = np.array([m @ cx for m in power])
    holt = np.zeros((P, CHUNK))
    for s in range(P):
        holt[s, s:] = hit[:CHUNK - s, 0]
    last = hit[CHUNK - 1::-1][:CHUNK].reshape(CT, P, 2).transpose(1, 0, 2)
    carry = np.array([power[t + 1][0] for t in range(CHUNK)]).T
    return holt, last.reshape(P, 2 * CT), carry, power[CHUNK].T


def kernel(**inputs):
    import concourse.bacc as bacc
    from concourse.bass_utils import run_bass_kernel_spmd

    v = {k: np.asarray(a) for k, a in inputs.items()}
    get = lambda name: v["L0_attn_" + name]
    packed = np.zeros((P, N_COLS), np.float32)

    def put(name, a):
        lo, hi = COLS[name]
        packed[:a.shape[0], lo:hi] = a.reshape(a.shape[0], hi - lo)

    def by_partition(a):
        return np.broadcast_to(a.reshape(1, -1), (P, a.size))

    put("wqk", np.stack([get(w + n).T for n in "12" for w in ("wk", "wq")], 1))
    put("bqk", np.stack([get(w + n) for n in "12" for w in ("bk", "bq")], 1))
    bv = np.zeros((GH, ROW, 2, GROUPS), np.float32)
    wo = np.zeros((GH, ROW, 2, GROUPS, DH), np.float32)
    for i, n in enumerate("12"):
        bv[:, :DK, i] = get("bv" + n).reshape(GROUPS, GH, DK).transpose(1, 2, 0)
        wo[:, :DK, i] = get("wo" + n).T.reshape(GROUPS, GH, DK, DH).transpose(1, 2, 0, 3)
    put("wv", np.stack([get("wv" + n).T for n in "12"], 1))
    put("bv", bv.reshape(P, -1))
    put("wo", wo.reshape(P, -1))
    put("bo", by_partition(np.concatenate([get("bo1"), get("bo2")])))
    put("gamma", by_partition(np.concatenate([get("g1"), get("g2")])))
    put("beta", by_partition(np.concatenate([get("be1"), get("be2")])))
    put("gamma_ff", by_partition(get("g_ff")))
    put("beta_ff", by_partition(get("be_ff")))
    put("b_ff2", by_partition(get("b_ff2")))
    put("b2", by_partition(v["L0_ffn_b2"]))
    put("b_ff1", get("b_ff1").reshape(HB, P).T)
    put("b1", v["L0_ffn_b1"].reshape(HB, P).T)
    put("ident", np.eye(P, dtype=np.float32))
    put("own", np.repeat(np.eye(HEADS, dtype=np.float32), DK, 0))
    for name, table in zip(("holt", "holt_state", "carry", "carry_state"), smoothing_tables()):
        put(name, table)

    def net(w1, w2):
        return np.concatenate([w1.reshape(2, P, FF).transpose(1, 0, 2).reshape(P, -1),
                               w2.reshape(HB, P, D).transpose(1, 0, 2).reshape(P, -1)], 1)

    arrays = {
        "x": np.ascontiguousarray(get("x")),
        "packed": packed,
        "w_ff": net(get("w_ff1").T, get("w_ff2").T),
        "w_ffn": net(v["L0_ffn_W1"], v["L0_ffn_W2"]),
    }
    nc = bacc.Bacc("TRN2", target_bir_lowering=False, num_devices=1)
    args = [nc.dram_tensor(k, a.shape, mybir.dt.from_np(a.dtype), kind="ExternalInput").ap() for k, a in arrays.items()]
    out = nc.dram_tensor("out", (B, S, D), mybir.dt.float32, kind="ExternalOutput").ap()
    build(nc, *args, out)
    return run_bass_kernel_spmd(nc, [arrays], core_ids=[0]).results[0]["out"]
```
